# Optimizing a Trainium2 kernel written in Bass

```python
import numpy as np
import jax
import jax.numpy as jnp

def _softmax(x, axis=-1):
    return jax.nn.softmax(x, axis=axis)

def _gelu(x):
    return jax.nn.gelu(x, approximate=True)

def _silu(x):
    return jax.nn.silu(x)

def _sigmoid(x):
    return jax.nn.sigmoid(x)

def _layernorm(x, axis=-1, eps=1e-05):
    m = jnp.mean(x, axis=axis, keepdims=True)
    v = jnp.var(x, axis=axis, keepdims=True)
    return (x - m) / jnp.sqrt(v + eps)

def _scatter_add(tgt, idx, src, axis=0):
    return tgt.at[idx].add(src)

def _segment_sum(src, seg, n):
    return jax.ops.segment_sum(src, seg, n)
kernel_name = 'mk_perceiver_d1_seqx_r8_81eca4'

def setup_inputs(seed: int=0):
    np.random.seed(seed)
    _w = jnp.asarray

    def _rec_inputs():
        import jax
        import jax.numpy as jnp
        _rk = jax.random.key(seed)
        x = -0.0002928 + 1 * jax.random.normal(jax.random.fold_in(_rk, 1), (1, 64, 128), jnp.float32)
        _lenS = 64 - jax.random.randint(jax.random.fold_in(_rk, 7), (1,), 0, max(1, 64 // 4) + 1, jnp.int32)
        _lenS2 = 6272 - jax.random.randint(jax.random.fold_in(_rk, 8), (1,), 0, max(1, 6272 // 4) + 1, jnp.int32)
        _ctx_768P = jax.random.normal(jax.random.fold_in(_rk, 11), (1, 16, 96), jnp.float32)
        _ctx_768c = jax.random.dirichlet(jax.random.fold_in(_rk, 511), 0.3 * jnp.ones((16,), jnp.float32), (1, 6272))
        _ctx_768t = jnp.einsum('bsk,bkd->bsd', _ctx_768c, _ctx_768P)
        _ctx_768t = _ctx_768t * jax.lax.rsqrt(jnp.mean(jnp.square(_ctx_768t)) + 1e-12) * 0.953939
        ctx_768 = 2.09791e-05 + 1.00001 * (_ctx_768t + 0.3 * jax.random.normal(jax.random.fold_in(_rk, 611), (1, 6272, 96), jnp.float32))
        return (x, ctx_768)
    x, ctx_768 = _rec_inputs()

    def _L0_xattn_setup():
        import jax, jax.numpy as jnp
        import numpy as np
        HEADS = 8
        DIM_HEAD = 128
        ATTN_MATRIX_SCALE = 1.5
        SCALE = DIM_HEAD ** (-0.5)

        def _split_heads(t):
            b, n, _ = t.shape
            t = t.reshape(b, n, HEADS, DIM_HEAD)
            return t.transpose(2, 0, 1, 3).reshape(HEADS, b * n, DIM_HEAD)
        key = jax.random.key(seed)
        ks = jax.random.split(key, 7)
        b, n, m = (2, 256, 256)
        qd, cd, inner = (128, 96, HEADS * DIM_HEAD)
        x = jax.random.normal(ks[0], (b, n, qd), dtype=jnp.float32)
        context = jax.random.normal(ks[1], (b, m, cd), dtype=jnp.float32)
        Wq = jax.random.normal(ks[2], (qd, inner), dtype=jnp.float32) * qd ** (-0.5)
        Wk = jax.random.normal(ks[3], (cd, inner), dtype=jnp.float32) * cd ** (-0.5)
        Wv = jax.random.normal(ks[4], (cd, inner), dtype=jnp.float32) * cd ** (-0.5)
        Wout = jax.random.normal(ks[5], (inner, qd), dtype=jnp.float32) * inner ** (-0.5)
        bout = jnp.zeros((qd,), dtype=jnp.float32)
        return {'x': x, 'context': context, 'Wq': Wq, 'Wk': Wk, 'Wv': Wv, 'Wout': Wout, 'bout': bout}
    _L0_xattn_all = _L0_xattn_setup()
    _L0_xattn_in = {k: v for k, v in _L0_xattn_all.items() if k in ('Wq', 'Wk', 'Wv', 'Wout', 'bout')}
    del _L0_xattn_all

    def _L0_attn_setup():
        import jax, jax.numpy as jnp
        import numpy as np
        NUM_HEADS = 16
        EPS = float(jnp.finfo(jnp.float32).eps)

        def rms_norm(x, w):
            ms = jnp.mean(x * x, axis=-1, keepdims=True)
            return x * jax.lax.rsqrt(ms + EPS) * w
        key = jax.random.key(seed)
        k = jax.random.split(key, 5)
        B, N, D = (4, 256, 128)
        Dh = D // NUM_HEADS
        return {'x': jax.random.normal(k[0], (B, N, D), dtype=jnp.float32), 'Wq': jax.random.normal(k[1], (D, D), dtype=jnp.float32) * 0.02, 'Wk': jax.random.normal(k[2], (D, D), dtype=jnp.float32) * 0.02, 'Wv': jax.random.normal(k[3], (D, D), dtype=jnp.float32) * 0.02, 'Wo': jax.random.normal(k[4], (D, D), dtype=jnp.float32) * 0.02, 'qn_w': jnp.ones((Dh,), dtype=jnp.float32), 'kn_w': jnp.ones((Dh,), dtype=jnp.float32)}
    _L0_attn_all = _L0_attn_setup()
    _L0_attn_in = {k: v for k, v in _L0_attn_all.items() if k in ('Wq', 'Wk', 'Wv', 'Wo', 'qn_w', 'kn_w')}
    del _L0_attn_all

    def _L0_ffn_setup():
        import jax, jax.numpy as jnp
        import numpy as np
        B, S, H = (2, 256, 128)
        F = 512
        E = 8
        TOP_K = 2
        SHARED_SCALE = 0.1
        EPS = 1e-09

        def _moe_forward(x3, Wg, W1, b1, W2, b2, Ws1, bs1, Ws2, bs2):
            b, s, h = x3.shape
            x = x3.reshape(-1, h)
            T = x.shape[0]
            logits = x @ Wg
            probs = jax.nn.softmax(logits, axis=-1)
            vals, idx = jax.lax.top_k(probs, TOP_K)
            weights = vals / (jnp.sum(vals, axis=-1, keepdims=True) + EPS)
            cw = jnp.zeros((T, E), dtype=x.dtype).at[jnp.arange(T)[:, None], idx].set(weights)
            hpre = jnp.einsum('th,ehf->tef', x, W1) + b1
            act = jax.nn.silu(hpre)
            y = jnp.einsum('tef,efh->teh', act, W2) + b2
            out = jnp.einsum('te,teh->th', cw, y)
            shared = jax.nn.silu(x @ Ws1 + bs1) @ Ws2 + bs2
            out = out + SHARED_SCALE * shared
            return out.reshape(b, s, h)
        key = jax.random.key(seed)
        ks = jax.random.split(key, 10)
        sc = 0.02
        return {'hidden_states': jax.random.normal(ks[0], (B, S, H), dtype=jnp.float32), 'Wg': jax.random.normal(ks[1], (H, E), dtype=jnp.float32) * sc, 'W1': jax.random.normal(ks[2], (E, H, F), dtype=jnp.float32) * sc, 'b1': jnp.zeros((E, F), dtype=jnp.float32), 'W2': jax.random.normal(ks[3], (E, F, H), dtype=jnp.float32) * sc, 'b2': jnp.zeros((E, H), dtype=jnp.float32), 'Ws1': jax.random.normal(ks[4], (H, F), dtype=jnp.float32) * sc, 'bs1': jnp.zeros((F,), dtype=jnp.float32), 'Ws2': jax.random.normal(ks[5], (F, H), dtype=jnp.float32) * sc, 'bs2': jnp.zeros((H,), dtype=jnp.float32)}
    _L0_ffn_all = _L0_ffn_setup()
    _L0_ffn_in = {k: v for k, v in _L0_ffn_all.items() if k in ('Wg', 'W1', 'b1', 'W2', 'b2', 'Ws1', 'bs1', 'Ws2', 'bs2')}
    del _L0_ffn_all
    return {'x': x, 'ctx_768': ctx_768, 'L0_xattn_Wq': _L0_xattn_in['Wq'], 'L0_xattn_Wk': _L0_xattn_in['Wk'], 'L0_xattn_Wv': _L0_xattn_in['Wv'], 'L0_xattn_Wout': _L0_xattn_in['Wout'], 'L0_xattn_bout': _L0_xattn_in['bout'], 'L0_attn_Wq': _L0_attn_in['Wq'], 'L0_attn_Wk': _L0_attn_in['Wk'], 'L0_attn_Wv': _L0_attn_in['Wv'], 'L0_attn_Wo': _L0_attn_in['Wo'], 'L0_attn_qn_w': _L0_attn_in['qn_w'], 'L0_attn_kn_w': _L0_attn_in['kn_w'], 'L0_ffn_Wg': _L0_ffn_in['Wg'], 'L0_ffn_W1': _L0_ffn_in['W1'], 'L0_ffn_b1': _L0_ffn_in['b1'], 'L0_ffn_W2': _L0_ffn_in['W2'], 'L0_ffn_b2': _L0_ffn_in['b2'], 'L0_ffn_Ws1': _L0_ffn_in['Ws1'], 'L0_ffn_bs1': _L0_ffn_in['bs1'], 'L0_ffn_Ws2': _L0_ffn_in['Ws2'], 'L0_ffn_bs2': _L0_ffn_in['bs2']}

def reference(x, ctx_768, L0_xattn_Wq, L0_xattn_Wk, L0_xattn_Wv, L0_xattn_Wout, L0_xattn_bout, L0_attn_Wq, L0_attn_Wk, L0_attn_Wv, L0_attn_Wo, L0_attn_qn_w, L0_attn_kn_w, L0_ffn_Wg, L0_ffn_W1, L0_ffn_b1, L0_ffn_W2, L0_ffn_b2, L0_ffn_Ws1, L0_ffn_bs1, L0_ffn_Ws2, L0_ffn_bs2):
    import jax
    import jax.numpy as jnp

    def _L0_xattn_ref(x, context, Wq, Wk, Wv, Wout, bout):
        import jax, jax.numpy as jnp
        import numpy as np
        HEADS = 8
        DIM_HEAD = 128
        ATTN_MATRIX_SCALE = 1.5
        SCALE = DIM_HEAD ** (-0.5)

        def _split_heads(t):
            b, n, _ = t.shape
            t = t.reshape(b, n, HEADS, DIM_HEAD)
            return t.transpose(2, 0, 1, 3).reshape(HEADS, b * n, DIM_HEAD)
        b, n, _ = x.shape
        qh = _split_heads(jnp.einsum('bnq,qi->bni', x, Wq))
        kh = _split_heads(jnp.einsum('bmc,ci->bmi', context, Wk))
        vh = _split_heads(jnp.einsum('bmc,ci->bmi', context, Wv))
        sim = jnp.einsum('hid,hjd->hij', qh, kh) * SCALE
        mean = jnp.mean(sim, axis=-1, keepdims=True)
        sim = (sim - mean) * ATTN_MATRIX_SCALE + mean
        attn = jax.nn.softmax(sim, axis=-1)
        out = jnp.einsum('hij,hjd->hid', attn, vh)
        out = out.reshape(HEADS, b, n, DIM_HEAD).transpose(1, 2, 0, 3)
        out = out.reshape(b, n, HEADS * DIM_HEAD)
        return jnp.einsum('bni,iq->bnq', out, Wout) + bout

    def _L0_attn_ref(x, Wq, Wk, Wv, Wo, qn_w, kn_w):
        import jax, jax.numpy as jnp
        import numpy as np
        NUM_HEADS = 16
        EPS = float(jnp.finfo(jnp.float32).eps)

        def rms_norm(x, w):
            ms = jnp.mean(x * x, axis=-1, keepdims=True)
            return x * jax.lax.rsqrt(ms + EPS) * w
        B, N, D = x.shape
        H = NUM_HEADS
        Dh = D // H
        scale = Dh ** (-0.5)

        def proj(W):
            return (x @ W.T).reshape(B, N, H, Dh).transpose(0, 2, 1, 3)
        q = rms_norm(proj(Wq), qn_w)
        k = rms_norm(proj(Wk), kn_w)
        v = proj(Wv)
        scores = jnp.einsum('bhnd,bhmd->bhnm', q, k) * scale
        attn = jax.nn.softmax(scores, axis=-1)
        out = jnp.einsum('bhnm,bhmd->bhnd', attn, v)
        out = out.transpose(0, 2, 1, 3).reshape(B, N, D)
        return out @ Wo.T

    def _L0_ffn_ref(hidden_states, Wg, W1, b1, W2, b2, Ws1, bs1, Ws2, bs2):
        import jax, jax.numpy as jnp
        import numpy as np
        B, S, H = (2, 256, 128)
        F = 512
        E = 8
        TOP_K = 2
        SHARED_SCALE = 0.1
        EPS = 1e-09

        def _moe_forward(x3, Wg, W1, b1, W2, b2, Ws1, bs1, Ws2, bs2):
            b, s, h = x3.shape
            x = x3.reshape(-1, h)
            T = x.shape[0]
            logits = x @ Wg
            probs = jax.nn.softmax(logits, axis=-1)
            vals, idx = jax.lax.top_k(probs, TOP_K)
            weights = vals / (jnp.sum(vals, axis=-1, keepdims=True) + EPS)
            cw = jnp.zeros((T, E), dtype=x.dtype).at[jnp.arange(T)[:, None], idx].set(weights)
            hpre = jnp.einsum('th,ehf->tef', x, W1) + b1
            act = jax.nn.silu(hpre)
            y = jnp.einsum('tef,efh->teh', act, W2) + b2
            out = jnp.einsum('te,teh->th', cw, y)
            shared = jax.nn.silu(x @ Ws1 + bs1) @ Ws2 + bs2
            out = out + SHARED_SCALE * shared
            return out.reshape(b, s, h)
        return _moe_forward(hidden_states, Wg, W1, b1, W2, b2, Ws1, bs1, Ws2, bs2)
    x = x + _L0_xattn_ref(_layernorm(x, axis=-1), ctx_768, L0_xattn_Wq, L0_xattn_Wk, L0_xattn_Wv, L0_xattn_Wout, L0_xattn_bout)
    x = x + _L0_attn_ref(_layernorm(x, axis=-1), L0_attn_Wq, L0_attn_Wk, L0_attn_Wv, L0_attn_Wo, L0_attn_qn_w, L0_attn_kn_w)
    x = x + _L0_ffn_ref(_layernorm(x, axis=-1), L0_ffn_Wg, L0_ffn_W1, L0_ffn_b1, L0_ffn_W2, L0_ffn_b2, L0_ffn_Ws1, L0_ffn_bs1, L0_ffn_Ws2, L0_ffn_bs2)
    return x

_drawn_inputs = setup_inputs


def setup_inputs(seed=0):
    import zlib

    import numpy as np

    out = dict(_drawn_inputs(seed))
    spreads = {'L0_xattn_bout': (0.0, 0.1),
     'L0_attn_qn_w': (1.0, 0.6),
     'L0_attn_kn_w': (1.0, 0.6),
     'L0_ffn_b1': (0.0, 0.593),
     'L0_ffn_b2': (0.0, 0.1),
     'L0_ffn_bs1': (0.0, 0.8),
     'L0_ffn_bs2': (0.0, 0.8)}
    factors = {'L0_attn_Wq': 7.429,
     'L0_attn_Wk': 7.352,
     'L0_attn_Wv': 2.875,
     'L0_ffn_Ws1': 8.0,
     'L0_ffn_Ws2': 8.0}
    for name, (base, spread) in spreads.items():
        noise = np.random.default_rng([zlib.crc32(name.encode()), seed]).standard_normal(out[name].shape)
        drawn = base * np.exp(spread * noise) if base else spread * noise
        out[name] = jnp.asarray(drawn.astype(out[name].dtype))
    for name, factor in factors.items():
        out[name] = (out[name] * factor).astype(out[name].dtype)
    return out
```

```python
from contextlib import ExitStack

import concourse.bass as bass
from concourse import mybir

F32 = mybir.dt.float32
F32R = mybir.dt.float32r
U32 = mybir.dt.uint32
ALU = mybir.AluOpType
ACT = mybir.ActivationFunctionType
AX = mybir.AxisListType

TOK, DM = 64, 128
KEYS, CD = 6272, 96
XH, XD = 8, 128
Q = XH * TOK
QB = Q // 128
TILE = 128
TPC = 7
CHUNK = TPC * TILE
NCH = KEYS // CHUNK
HALF = CHUNK // 2
XSCALE = 1.5 * XD ** -0.5
SH, SD = 16, 8
NE, FF = 8, 512
FC = FF // 128
EPB = 2
NB = NE // EPB
LN_EPS, RMS_EPS, W_EPS, SHARED = 1e-5, 1.1920928955078125e-07, 1e-9, 0.1
LOWEST = -3.0e38

C_ID, C_MR, C_ML, C_MV, C_IO = 0, 128, 136, 138, 146
C_W = 154


def build(nc, x, ctx_n, ctx_t, wq_t, wk_t, wv_t, wout, bout, wqkv, wo_t, norm_w, wg, w1, w2, ws1, ws2,
          b1_rows, bs1_rows, b2_rows, consts, sel8, out):
    with ExitStack() as ctx:
        def sb(name, shape, dt=F32):
            return ctx.enter_context(nc.sbuf_tensor(name, shape, dt))

        def pb(name, shape, dt=F32):
            return ctx.enter_context(nc.psum_tensor(name, shape, dt))

        def sem(name):
            return ctx.enter_context(nc.semaphore(name))

        x_sb = sb("x_sb", [TOK, DM])
        xb = sb("xb", [TOK, DM])
        bout_b = sb("bout_b", [TOK, DM])
        cst = sb("cst", [128, C_W])
        ident_r = sb("ident_r", [128, 128], F32R)
        expo = sb("expo", [128, 32])
        wqT = sb("wqT", [128, XH, DM])
        wkT = sb("wkT", [128, XH, CD])
        wvT = sb("wvT", [128, XH, CD])
        wo_x = sb("wo_x", [128, XH, DM])
        A = sb("A", [128, XH, CD])
        Bm = sb("Bm", [CD + 1, XH, DM + 1])
        ctx32 = [sb(f"ctx32_{p}", [CD, CHUNK]) for p in range(2)]
        ctx_hi = [sb(f"ctx_hi_{p}", [CD + 1, CHUNK], F32R) for p in range(2)]
        ctx_lo = [sb(f"ctx_lo_{p}", [CD, CHUNK], F32R) for p in range(2)]
        val = [sb(f"val_{p}", [128, TPC, CD + 1]) for p in range(2)]
        q_hi = [sb(f"q_hi_{p}", [CD + 1, Q], F32R) for p in range(2)]
        q_lo = sb("q_lo", [CD, Q], F32R)
        mx = sb("mx", [128, QB])
        m_run = [sb(f"m_run_{p}", [128, QB], F32R) for p in range(2)]
        m_row = [sb(f"m_row_{p}", [CD + 1, Q]) for p in range(2)]
        m_diff = sb("m_diff", [CD + 1, Q])
        alpha = sb("alpha", [CD + 1, Q])
        probs = [sb(f"probs_{i}", [128, Q]) for i in range(3)]
        acc = sb("acc", [CD + 1, Q])
        st = sb("st", [TOK, 6])
        mv = sb("mv", [TOK, 2])
        ve = sb("ve", [TOK, 1])
        rstd = sb("rstd", [TOK, 1])
        xn = sb("xn", [TOK, DM])
        xnT = sb("xnT", [DM, 2 * TOK])
        xr = [sb(f"xr_{i}", [TOK, DM]) for i in range(2)]
        x1 = sb("x1", [TOK, DM])
        rs_x = sb("rs_x", [TOK, XH])
        wqkv_sb = sb("wqkv_sb", [DM, 3 * DM])
        woT_sb = sb("woT_sb", [DM // 2, 2, DM])
        nw = sb("nw", [128, 2])
        wn = sb("wn", [128, 1])
        wmask = sb("wmask", [128, 2])
        sq = sb("sq", [TOK, 2 * DM])
        ms = sb("ms", [TOK, 2 * SH])
        mse = sb("mse", [TOK, 2 * SH])
        rr = sb("rr", [TOK, 2 * SH])
        qkn = sb("qkn", [TOK, 2 * DM])
        qm = sb("qm", [128, 2, TOK])
        km = sb("km", [128, 8, TOK])
        vm = sb("vm", [128, 8, 17])
        smax = sb("smax", [128, 8])
        sd = sb("sd", [128, 8, TOK])
        pe_ = sb("pe_", [128, 8, TOK])
        pT = sb("pT", [128, 4, 128])
        rsum = sb("rsum", [128, 8])
        ao = sb("ao", [128, 8, 8])
        aoT = sb("aoT", [DM // 2, 2, TOK])
        x2 = sb("x2", [TOK, DM])
        wg_sb = sb("wg_sb", [DM, NE])
        w1_sb = sb("w1_sb", [DM, NE + 1, FF])
        w2_sb = sb("w2_sb", [128, NE + 1, FC, DM])
        b1_sb = sb("b1_sb", [8, NB + 1, 128])
        b2_sb = sb("b2_sb", [NE + 1, DM])
        sel_sb = sb("sel_sb", [8, 8 * TOK])
        halves = sb("halves", [TOK, 128])
        nlm = sb("nlm", [TOK, 1])
        le = sb("le", [TOK, NE])
        ls = sb("ls", [TOK, 1])
        lr = sb("lr", [TOK, 1])
        pr = sb("pr", [TOK, NE])
        v8 = sb("v8", [TOK, 8])
        i8 = sb("i8", [TOK, 8], U32)
        if8 = sb("if8", [TOK, 2])
        wsum = sb("wsum", [TOK, 1])
        wr = sb("wr", [TOK, 1])
        w2v = sb("w2v", [TOK, 2])
        c1 = sb("c1", [TOK, NE])
        c2 = sb("c2", [TOK, NE])
        cw = sb("cw", [TOK, NE + 1])
        cwd = sb("cwd", [TOK, NE, TOK])
        cwT = sb("cwT", [NE + 1, TOK])
        th = [sb(f"th_{b}", [128, 8 * TOK]) for b in range(NB + 1)]
        hs = [sb(f"hs_{b}", [128, 8 * TOK]) for b in range(NB + 1)]
        hw = [sb(f"hw_{b}", [128, 8 * TOK]) for b in range(NB)]
        yT = sb("yT", [DM, TOK])
        y = sb("y", [TOK, DM])

        PM = pb("PM", [128, 2, 2, 512])
        PS = pb("PS", [128, 2, 512])
        PO = pb("PO", [128, 2, 512])

        s_x = sem("x_loaded")
        s_cst = sem("consts_loaded")
        s_bout = sem("bout_loaded")
        s_wq = sem("wq_loaded")
        s_wk = sem("wk_loaded")
        s_wv = sem("wv_wout_loaded")
        s_aw = sem("attn_weights_loaded")
        s_fw1 = sem("w1_loaded")
        s_fw2 = sem("w2_loaded")
        s_fb = sem("ffn_small_loaded")
        s_ct = [sem(f"ctx32_{p}_loaded") for p in range(2)]
        s_cv = [sem(f"val_{p}_loaded") for p in range(2)]
        s_ones = sem("constants_set")
        s_dz = sem("vector_constants_set")
        s_idr = sem("ident_rounded")
        s_ve = sem("variance_ready")
        s_pow = sem("inverse_root_ready")
        s_xn = sem("normed_ready")
        s_xnT_ps = sem("normed_transposed")
        s_xnT = sem("normed_T_ready")
        s_A_ps = sem("A_in_psum")
        s_A = sem("A_ready")
        s_B_ps = sem("B_in_psum")
        s_B = sem("B_ready")
        s_q_ps = sem("queries_in_psum")
        s_qh = sem("q_hi_ready")
        s_ql = sem("q_lo_ready")
        s_hi = sem("ctx_hi_ready")
        s_lo = sem("ctx_lo_ready")
        s_mm = sem("max_scores_ready")
        s_mr = sem("max_reduced")
        s_run = sem("running_max_ready")
        s_bc = sem("max_broadcast_ready")
        s_row = sem("shift_row_ready")
        s_mb = sem("max_row_copied")
        s_df = sem("max_diff_ready")
        s_al = sem("alpha_ready")
        s_sc = sem("scores_ready")
        s_ex = sem("probs_ready")
        s_pv = sem("tile_summed")
        s_am = sem("acc_scaled")
        s_cb = sem("chunk_combined")
        s_y = sem("heads_projected")
        s_x1 = sem("x1_ready")
        s_dve = sem("vector_step")
        s_qkv = sem("qkv_in_psum")
        s_sq = sem("squares_ready")
        s_mse = sem("mean_squares_ready")
        s_qkn = sem("qk_normed")
        s_qkT = sem("qk_transposed")
        s_qm = sem("q_masked")
        s_km = sem("k_masked")
        s_vm = sem("v_masked")
        s_ss = sem("self_scores_ready")
        s_sd = sem("self_scores_shifted")
        s_sp = sem("self_probs_ready")
        s_pt = sem("self_probs_transposed")
        s_ptc = sem("self_probs_T_ready")
        s_so = sem("self_sums_ready")
        s_ao = sem("self_out_ready")
        s_aoT = sem("self_out_transposed")
        s_aoTc = sem("self_out_T_ready")
        s_pj = sem("self_projected")
        s_x2 = sem("x2_ready")
        s_lg = sem("logits_ready")
        s_nl = sem("logit_max_ready")
        s_le = sem("logit_exp_ready")
        s_cw = sem("gates_ready")
        s_cwT = sem("gates_transposed")
        s_cwTc = sem("gates_T_ready")
        s_cwd = sem("gates_diagonal_ready")
        s_cwb = sem("gates_broadcast")
        s_ws2 = sem("ws2_scaled")
        s_hid = sem("hidden_ready")
        s_th = sem("tanh_ready")
        s_hs = sem("silu_ready")
        s_hw = sem("weighted_ready")
        s_yT = sem("yT_in_psum")
        s_yTc = sem("yT_ready")
        s_yn = sem("y_in_psum")
        s_fin = sem("result_ready")
        s_out = sem("result_stored")

        ident = cst[:, C_ID:C_ID + 128]
        block = ctx.enter_context(nc.Block())

        def follow(i, k):
            return (i, 1) if k == 0 else (i + 1, 0)

        def number(i, k):
            return 2 * i + k

        @block.sync
        def _(sp):
            sp.dma_start(x_sb[:, :], x).then_inc(s_x, 16)
            sp.dma_start(wkT[:, :, :], wk_t).then_inc(s_wk, 16)
            sp.dma_start(ctx32[0][:, :], ctx_t[:, 0, :]).then_inc(s_ct[0], 16)
            sp.dma_start(bout_b[:, :], bout.rearrange("(a n) -> a n", a=1).to_broadcast([TOK, DM])).then_inc(s_bout, 16)
            sp.dma_start(wvT[:, :, :], wv_t).then_inc(s_wv, 16)
            sp.dma_start(wo_x[:, :, :], wout).then_inc(s_wv, 16)
            sp.dma_start(val[0][:, :, 0:CD], ctx_n[0]).then_inc(s_cv[0], 16)
            sp.dma_start(ctx32[1][:, :], ctx_t[:, 1, :]).then_inc(s_ct[1], 16)
            sp.dma_start(val[1][:, :, 0:CD], ctx_n[1]).then_inc(s_cv[1], 16)
            sp.dma_start(wqkv_sb[:, :], wqkv).then_inc(s_aw, 16)
            sp.dma_start(woT_sb[:, :, :], wo_t).then_inc(s_aw, 16)
            sp.dma_start(nw[:, :], norm_w).then_inc(s_aw, 16)
            sp.dma_start(wg_sb[:, :], wg).then_inc(s_fb, 16)
            sp.dma_start(b1_sb[:, 0:NB, :], b1_rows).then_inc(s_fb, 16)
            sp.dma_start(b1_sb[0:FC, NB, :], bs1_rows).then_inc(s_fb, 16)
            sp.dma_start(b2_sb[:, :], b2_rows).then_inc(s_fb, 16)
            sp.dma_start(sel_sb[:, :], sel8).then_inc(s_fb, 16)
            sp.dma_start(w2_sb[:, NE, :, :], ws2).then_inc(s_fw2, 16)

            def load(i, k, c):
                sp.wait_ge(s_lo, c - 1)
                sp.dma_start(ctx32[k][:, :], ctx_t[:, c, :]).then_inc(s_ct[k], 16)
                sp.wait_ge(s_pv, TPC * (c - 1))
                sp.dma_start(val[k][:, :, 0:CD], ctx_n[c]).then_inc(s_cv[k], 16)

            load(1, 0, 2)
            sp.dma_start(w1_sb[:, 0:NE, :], w1).then_inc(s_fw1, 16)
            sp.dma_start(w1_sb[:, NE, :], ws1).then_inc(s_fw1, 16)
            sp.dma_start(w2_sb[:, 0:NE, :, :], w2).then_inc(s_fw2, 16)
            load(1, 1, 3)
            load(2, 0, 4)
            load(2, 1, 5)
            load(3, 0, 6)
            sp.wait_ge(s_fin, 1)
            sp.dma_start(out, y[:, :]).then_inc(s_out, 16)
            sp.wait_ge(s_out, 16)

        @block.gpsimd
        def _(pool):
            fills = [(expo[:, :], -0.5), (Bm[:, :, :], 0.0), (Bm[CD:CD + 1, :, DM:DM + 1], 1.0), (halves[:, :], 0.5),
                     (cw[:, NE:NE + 1], SHARED), (vm[:, :, 16:17], 0.0)]
            for p in range(2):
                fills += [(ctx_hi[p][CD:CD + 1, :].bitcast(F32), 1.0), (val[p][:, :, CD:CD + 1], 1.0)]
            for n, (place, value) in enumerate(fills):
                pool.memset(place, value).then_inc(s_ones, 1)
                pool.wait_ge(s_ones, n + 1)

            def inverse_root(n, dst, src, width):
                pool.wait_ge(s_ve, n)
                pool.tensor_tensor(dst, src, expo[0:TOK, 0:width], ALU.pow).then_inc(s_pow, 1)

            def low_part(i, k, c):
                pool.wait_ge(s_hi, c + 1)
                if c >= 2:
                    pool.wait_ge(s_sc, TPC * (c - 1))
                pool.tensor_tensor(ctx_lo[k][:, :], ctx32[k][:, :], ctx_hi[k][0:CD, :].bitcast(F32),
                                   ALU.subtract).then_inc(s_lo, 1)

            inverse_root(1, rstd[:, :], ve[:, :], 1)
            for c in range(NCH):
                low_part(c // 2, c % 2, c)
            inverse_root(2, rstd[:, :], ve[:, :], 1)
            pool.wait_ge(s_mse, 1)
            pool.tensor_tensor(rr[:, :], mse[:, :], expo[0:TOK, :], ALU.pow).then_inc(s_pow, 1)
            inverse_root(3, rstd[:, :], ve[:, :], 1)

        @block.scalar
        def _(act):
            act.dma_start(wqT[:, :, :], wq_t).then_inc(s_wq, 16)
            act.dma_start(cst[:, :], consts).then_inc(s_cst, 16)
            for j in range(2):
                act.wait_ge(s_A_ps, j + 1)
                act.activation(A[:, 4 * j:4 * j + 4, :], PS[:, j, 0:4 * CD].rearrange("p (h c) -> p h c", h=4),
                               ACT.Copy, scale=XSCALE).then_inc(s_A, 1)
            act.wait_ge(s_q_ps, 1)
            act.activation(q_hi[0][0:CD, :], PO[0:CD, 0, :], ACT.Copy).then_inc(s_qh, 1)
            act.wait_ge(s_qh, 1)
            act.activation(q_hi[1][0:CD, :], q_hi[0][0:CD, :].bitcast(F32), ACT.Copy).then_inc(s_qh, 1)
            act.wait_ge(s_ones, 10)
            for j in range(2):
                act.wait_ge(s_B_ps, j + 1)
                act.activation(Bm[0:CD, 4 * j:4 * j + 4, 0:DM], PS[0:CD, j, :].rearrange("p (h c) -> p h c", h=4),
                               ACT.Copy).then_inc(s_B, 1)

            def max_rows(i, k, c):
                act.wait_ge(s_bc, c + 1)
                if c >= 2:
                    act.wait_ge(s_sc, TPC * (c - 1))
                    act.wait_ge(s_df, c)
                act.activation(q_hi[k][CD:CD + 1, :], PM[CD:CD + 1, 0, 0, :], ACT.Copy, scale=-1.0).then_inc(s_row, 1)
                act.activation(m_row[k][:, :], PM[0:CD + 1, 0, 0, :], ACT.Copy).then_inc(s_mb, 1)

            def exps(i, k, c):
                for t in range(TPC):
                    act.wait_ge(s_sc, TPC * c + t + 1)
                    n = TPC * c + t
                    if n >= 3:
                        act.wait_ge(s_pv, n - 2)
                    act.activation(probs[n % 3][:, :], PS[:, n % 2, :], ACT.Exp).then_inc(s_ex, 1)
                    if t == 1:
                        act.wait_ge(s_df, c + 1)
                        if c >= 1:
                            act.wait_ge(s_am, c)
                        act.activation(alpha[:, :], m_diff[:, :], ACT.Exp).then_inc(s_al, 1)

            max_rows(0, 0, 0)
            for c in range(NCH):
                exps(c // 2, c % 2, c)
                if c + 1 < NCH:
                    max_rows((c + 1) // 2, (c + 1) % 2, c + 1)

            act.wait_ge(s_fw2, 32)
            act.activation(w2_sb[:, NE, :, :], w2_sb[:, NE, :, :], ACT.Copy, scale=0.5 * SHARED).then_inc(s_ws2, 1)
            act.wait_ge(s_qkv, 1)
            act.activation(sq[:, :], PO[0:TOK, 0, 0:2 * DM], ACT.Square).then_inc(s_sq, 1)
            act.wait_ge(s_sd, 1)
            act.activation(pe_[:, :, :], sd[:, :, :], ACT.Exp).then_inc(s_sp, 1)
            act.wait_ge(s_nl, 1)
            act.activation(le[:, :], PO[0:TOK, 0, 384:384 + NE], ACT.Exp, bias=nlm[:, 0:1],
                           accum_out=ls[:, :]).then_inc(s_le, 1)
            for n, b in enumerate([NB] + list(range(NB))):
                w = FC * TOK if b == NB else 8 * TOK
                src = PS[:, 0, 0:w] if b == NB else PM[:, b // 2, b % 2, :]
                act.wait_ge(s_hid, n + 1)
                act.activation(th[b][:, 0:w], src, ACT.Tanh, scale=0.5).then_inc(s_th, 1)

        @block.vector
        def _(dve):
            steps = [0]

            def link(ins):
                steps[0] += 1
                ins.then_inc(s_dve, 1)
                dve.wait_ge(s_dve, steps[0])

            def layer_norm(n, src, copies):
                link(dve.bn_stats(st[:, :], src[:, :]))
                link(dve.bn_aggr(mv[:, :], st[:, :]))
                dve.tensor_scalar(ve[:, :], mv[:, 1:2], LN_EPS, None, ALU.add).then_inc(s_ve, 1)
                dve.wait_ge(s_pow, [1, 2, 4][n - 1])
                dve.tensor_scalar(xn[:, :], src[:, :], mv[:, 0:1], rstd[:, 0:1], ALU.subtract,
                                  ALU.mult).then_inc(s_xn, 1)
                dve.wait_ge(s_xnT_ps, n)
                if copies == 2:
                    dve.tensor_copy(xnT[:, :].rearrange("p (a t) -> p a t", a=2),
                                    PO[:, 1, None, 0:TOK].to_broadcast([128, 2, TOK])).then_inc(s_xnT, 1)
                else:
                    dve.tensor_copy(xnT[:, 0:TOK], PO[:, 1, 0:TOK]).then_inc(s_xnT, 1)

            dve.memset(m_run[1][:, :].bitcast(F32), LOWEST).then_inc(s_dz, 1)
            dve.memset(m_row[1][:, :], LOWEST).then_inc(s_dz, 1)
            dve.memset(acc[:, :], 0.0).then_inc(s_dz, 1)
            dve.wait_ge(s_x, 16)
            layer_norm(1, x_sb, 1)

            def high_part(i, k, c):
                dve.wait_ge(s_ct[k], 16 * (i + 1))
                if c >= 2:
                    dve.wait_ge(s_sc, TPC * (c - 1))
                dve.tensor_copy(ctx_hi[k][0:CD, :], ctx32[k][:, :]).then_inc(s_hi, 1)

            def maxima(i, k, c):
                for b in range(QB):
                    dve.wait_ge(s_mm, QB * c + b + 1)
                    dve.tensor_reduce(mx[:, b:b + 1], PM[:, b % 2, :, 0:HALF], AX.XY, ALU.max).then_inc(s_mr, 1)
                dve.wait_ge(s_mr, QB * (c + 1))
                if c >= 2:
                    dve.wait_ge(s_bc, c - 1)
                dve.tensor_tensor(m_run[k][:, :], mx[:, :], m_run[1 - k][:, :].bitcast(F32),
                                  ALU.max).then_inc(s_run, 1)
                dve.wait_ge(s_mb, c + 1)
                if c >= 1:
                    dve.wait_ge(s_al, c)
                dve.tensor_tensor(m_diff[:, :], m_row[1 - k][:, :], m_row[k][:, :], ALU.subtract).then_inc(s_df, 1)

            def combine(i, k, c):
                dve.wait_ge(s_al, c + 1)
                dve.tensor_tensor(acc[:, :], acc[:, :], alpha[:, :], ALU.mult).then_inc(s_am, 1)
                dve.wait_ge(s_am, c + 1)
                dve.wait_ge(s_pv, TPC * (c + 1))
                dve.tensor_tensor(acc[:, :], acc[:, :], PO[0:CD + 1, k, :], ALU.add).then_inc(s_cb, 1)
                dve.wait_ge(s_cb, c + 1)

            dve.wait_ge(s_cst, 16)
            dve.tensor_copy(ident_r[:, :], ident).then_inc(s_idr, 1)
            high_part(0, 0, 0)
            dve.wait_ge(s_qh, 1)
            dve.tensor_tensor(q_lo[:, :], PO[0:CD, 0, :], q_hi[0][0:CD, :].bitcast(F32), ALU.subtract).then_inc(s_ql, 1)
            dve.wait_ge(s_dz, 3)
            maxima(0, 0, 0)
            for c in range(NCH):
                n = c + 1
                if n < NCH:
                    high_part(n // 2, n % 2, n)
                if n < NCH:
                    maxima(n // 2, n % 2, n)
                if c == 1:
                    dve.wait_ge(s_bout, 16)
                    dve.tensor_tensor(xb[:, :], x_sb[:, :], bout_b[:, :], ALU.add).then_inc(s_dz, 1)
                    dve.wait_ge(s_aw, 48)
                    link(dve.tensor_tensor(wn[:, :], nw[:, 0:1], nw[:, 1:2], ALU.mult))
                    link(dve.tensor_scalar(wmask[:, :], cst[:, C_ML:C_ML + 2], wn[:, 0:1], SD ** -0.5, ALU.mult,
                                           ALU.mult))
                combine(c // 2, c % 2, c)

            dve.wait_ge(s_dz, 4)
            src = xb
            for h in range(XH):
                Y = PM[0:TOK, h // 4, (h // 2) % 2, 256 * (h % 2):256 * (h % 2) + DM + 1]
                if h % 2 == 0:
                    dve.wait_ge(s_y, h // 2 + 1)
                    two = PM[0:TOK, h // 4, (h // 2) % 2, :].rearrange("p (a c) -> p a c", a=2)[:, :, DM]
                    link(dve.reciprocal(rs_x[:, h:h + 2], two))
                dst = x1 if h == XH - 1 else xr[h % 2]
                ins = dve.scalar_tensor_tensor(out=dst[:, :], in0=Y[:, 0:DM], scalar=rs_x[:, h:h + 1], in1=src[:, :],
                                               op0=ALU.mult, op1=ALU.add)
                if h == XH - 1:
                    ins.then_inc(s_x1, 1)
                    dve.wait_ge(s_x1, 1)
                else:
                    link(ins)
                src = dst

            layer_norm(2, x1, 2)
            dve.wait_ge(s_sq, 1)
            link(dve.tensor_reduce(ms[:, :], sq[:, :].rearrange("p (g d) -> p g d", d=SD), AX.X, ALU.add))
            dve.tensor_scalar(mse[:, :], ms[:, :], 1.0 / SD, RMS_EPS, ALU.mult, ALU.add).then_inc(s_mse, 1)
            dve.wait_ge(s_ones, 10)
            dve.tensor_tensor(vm[:, :, 0:16], PO[:, 0, 2 * DM:3 * DM].rearrange("p (g e) -> p g e", e=16),
                              cst[:, C_MV:C_MV + 8, None].to_broadcast([128, 8, 16]), ALU.mult).then_inc(s_vm, 1)
            dve.tensor_copy(vm[:, :, 16], cst[:, C_MV:C_MV + 8]).then_inc(s_vm, 1)
            dve.wait_ge(s_pow, 3)
            dve.tensor_tensor(qkn[:, :].rearrange("p (g d) -> p g d", d=SD),
                              PO[0:TOK, 0, 0:2 * DM].rearrange("p (g d) -> p g d", d=SD),
                              rr[:, :, None].to_broadcast([TOK, 2 * SH, SD]), ALU.mult).then_inc(s_qkn, 1)
            dve.wait_ge(s_qkT, 1)
            dve.tensor_tensor(qm[:, :, :], PO[:, 1, None, 64:128].to_broadcast([128, 2, TOK]),
                              wmask[:, :, None].to_broadcast([128, 2, TOK]), ALU.mult).then_inc(s_qm, 1)
            for j in range(2):
                dve.tensor_tensor(km[:, 4 * j:4 * j + 4, :], PO[:, 1, None, 128:192].to_broadcast([128, 4, TOK]),
                                  cst[:, C_MR + 4 * j:C_MR + 4 * j + 4, None].to_broadcast([128, 4, TOK]),
                                  ALU.mult).then_inc(s_km, 1)
            dve.wait_ge(s_ss, 1)
            S = PS[:, 0, :].rearrange("p (g m) -> p g m", g=8)
            link(dve.tensor_reduce(smax[:, :], S, AX.X, ALU.max))
            dve.tensor_tensor(sd[:, :, :], S, smax[:, :, None].to_broadcast([128, 8, TOK]), ALU.subtract).then_inc(s_sd, 1)
            dve.wait_ge(s_pt, 1)
            dve.tensor_copy(pT[:, :, :], PS[:, 1, :].rearrange("p (g m) -> p g m", g=4)).then_inc(s_ptc, 1)
            dve.wait_ge(s_so, 1)
            O = PO[:, 0, 0:8 * 17].rearrange("p (g e) -> p g e", e=17)
            link(dve.reciprocal(rsum[:, :], O[:, :, 16]))
            for a in range(2):
                rows = slice(TOK * a, TOK * a + TOK)
                dve.tensor_tensor(ao[rows, :, :], O[rows, :, SD * a:SD * a + SD],
                                  rsum[rows, :, None].to_broadcast([TOK, 8, SD]), ALU.mult).then_inc(s_ao, 1)
            dve.wait_ge(s_aoT, 1)
            dve.tensor_copy(aoT[:, :, :], PO[0:DM // 2, 1, 192:320].rearrange("p (a t) -> p a t", a=2)).then_inc(s_aoTc, 1)
            dve.wait_ge(s_pj, 1)
            dve.tensor_tensor(x2[:, :], x1[:, :], PO[0:TOK, 0, 256:384], ALU.add).then_inc(s_x2, 1)
            dve.wait_ge(s_x2, 1)

            layer_norm(3, x2, 1)
            dve.wait_ge(s_lg, 1)
            dve.tensor_reduce(nlm[:, :], PO[0:TOK, 0, 384:384 + NE], AX.X, ALU.max, negate=True).then_inc(s_nl, 1)
            dve.wait_ge(s_le, 1)
            link(dve.reciprocal(lr[:, :], ls[:, :]))
            link(dve.tensor_scalar(pr[:, :], le[:, :], lr[:, 0:1], None, ALU.mult))
            link(dve.max(v8[:, :], pr[:, :]))
            dve.max_index(i8[:, :], v8[:, :], pr[:, :]).then_inc(s_dve, 1)
            steps[0] += 1
            link(dve.tensor_scalar(wsum[:, :], v8[:, 0:1], v8[:, 1:2], W_EPS, ALU.add, ALU.add))
            link(dve.reciprocal(wr[:, :], wsum[:, :]))
            dve.tensor_copy(if8[:, :], i8[:, 0:2]).then_inc(s_dve, 1)
            steps[0] += 1
            link(dve.tensor_scalar(w2v[:, :], v8[:, 0:2], wr[:, 0:1], None, ALU.mult))
            dve.tensor_scalar(c1[:, :], cst[0:TOK, C_IO:C_IO + NE], if8[:, 0:1], w2v[:, 0:1], ALU.is_equal,
                              ALU.mult).then_inc(s_dve, 1)
            steps[0] += 1
            link(dve.tensor_scalar(c2[:, :], cst[0:TOK, C_IO:C_IO + NE], if8[:, 1:2], w2v[:, 1:2], ALU.is_equal,
                                   ALU.mult))
            dve.tensor_tensor(cw[:, 0:NE], c1[:, :], c2[:, :], ALU.add).then_inc(s_cw, 1)
            dve.wait_ge(s_cw, 1)
            dve.tensor_tensor(cwd[:, :, :], cst[0:TOK, None, C_ID:C_ID + TOK].to_broadcast([TOK, NE, TOK]),
                              cw[:, 0:NE, None].to_broadcast([TOK, NE, TOK]), ALU.mult).then_inc(s_cwd, 1)

            def silu(n, b, w, src):
                dve.wait_ge(s_th, n + 1)
                dve.scalar_tensor_tensor(out=hs[b][:, 0:w], in0=th[b][:, 0:w], scalar=1.0, in1=src,
                                         op0=ALU.add, op1=ALU.mult).then_inc(s_hs, 1)

            silu(0, NB, FC * TOK, PS[:, 0, 0:FC * TOK])
            dve.wait_ge(s_cwT, 1)
            dve.tensor_copy(cwT[:, :], PO[0:NE + 1, 0, 0:TOK]).then_inc(s_cwTc, 1)
            for b in range(NB):
                silu(b + 1, b, 8 * TOK, PM[:, b // 2, b % 2, :])
                dve.wait_ge(s_hs, b + 2)
                dve.wait_ge(s_cwb, 1)
                cwb = PS[:, 1, :].rearrange("p (e t) -> p e t", e=NE)[:, EPB * b:EPB * b + EPB, None, :]
                dve.tensor_tensor(hw[b][:, :].rearrange("p (e f t) -> p e f t", e=EPB, f=FC),
                                  hs[b][:, :].rearrange("p (e f t) -> p e f t", e=EPB, f=FC),
                                  cwb.to_broadcast([128, EPB, FC, TOK]), ALU.mult).then_inc(s_hw, 1)
            dve.wait_ge(s_yT, 1)
            dve.tensor_copy(yT[:, :], PO[:, 1, 320:320 + TOK]).then_inc(s_yTc, 1)
            dve.wait_ge(s_yn, 1)
            dve.tensor_tensor(y[:, :], x2[:, :], PO[0:TOK, 0, 128:256], ALU.add).then_inc(s_fin, 1)

        @block.tensor
        def _(pe):
            def transpose_normed(n):
                pe.wait_ge(s_xn, n)
                pe.transpose(PO[:, 1, 0:TOK], xn[:, :], ident[0:TOK, 0:TOK]).then_inc(s_xnT_ps, 1)

            pe.wait_ge(s_wq, 16)
            pe.wait_ge(s_wk, 16)
            for j in range(2):
                for h in range(4 * j, 4 * j + 4):
                    last = pe.matmul(PS[:, j, CD * (h % 4):CD * (h % 4) + CD], wqT[:, h, :], wkT[:, h, :],
                                     start=True, stop=True)
                last.then_inc(s_A_ps, 1)
            pe.wait_ge(s_cst, 16)
            transpose_normed(1)
            pe.wait_ge(s_xnT, 1)
            for h in range(XH):
                if h % 4 == 0:
                    pe.wait_ge(s_A, h // 4 + 1)
                last = pe.matmul(PO[0:CD, 0, TOK * h:TOK * h + TOK], A[:, h, :], xnT[:, 0:TOK], start=True, stop=True)
            last.then_inc(s_q_ps, 1)

            def max_block(k, c, b):
                if b == 0:
                    pe.wait_ge(s_hi, c + 1)
                    if c >= 1:
                        pe.wait_ge(s_row, c)
                        pe.wait_ge(s_mb, c)
                if QB * c + b >= 2:
                    pe.wait_ge(s_mr, QB * c + b - 1)
                for j in range(2):
                    last = pe.matmul(PM[:, b % 2, j, 0:HALF], q_hi[0][0:CD, 128 * b:128 * b + 128],
                                     ctx_hi[k][0:CD, HALF * j:HALF * j + HALF], start=True, stop=True)
                last.then_inc(s_mm, 1)

            def max_broadcast(k, c):
                pe.wait_ge(s_run, c + 1)
                for b in range(QB):
                    last = pe.matmul(PM[:, 0, 0, 128 * b:128 * b + 128], m_run[k][:, b:b + 1].to_broadcast([128, 128]),
                                     ident_r[:, :], start=True, stop=True)
                last.then_inc(s_bc, 1)

            def score(k, c, t, n):
                if t == 0:
                    pe.wait_ge(s_hi, c + 1)
                    pe.wait_ge(s_lo, c + 1)
                    pe.wait_ge(s_row, c + 1)
                if n >= 2:
                    pe.wait_ge(s_ex, n - 1)
                keys = slice(TILE * t, TILE * t + TILE)
                S = PS[:, n % 2, :]
                pe.matmul(S, ctx_hi[k][:, keys], q_hi[k][:, :], start=True, stop=False)
                pe.matmul(S, ctx_hi[k][0:CD, keys], q_lo[:, :], start=False, stop=False)
                pe.matmul(S, ctx_lo[k][:, keys], q_hi[k][0:CD, :], start=False, stop=True).then_inc(s_sc, 1)

            def sum_values(i, k, c, t, n):
                if t == 0:
                    pe.wait_ge(s_cv[k], 16 * (i + 1))
                    if c >= 2:
                        pe.wait_ge(s_cb, c - 1)
                pe.wait_ge(s_ex, n + 1)
                pe.matmul(PO[0:CD + 1, k, :], val[k][:, t, :], probs[n % 3][:, :],
                          start=(t == 0), stop=(t == TPC - 1)).then_inc(s_pv, 1)

            pe.wait_ge(s_ones, 10)
            pe.wait_ge(s_idr, 1)
            pe.wait_ge(s_qh, 1)
            pe.wait_ge(s_ql, 1)
            max_block(0, 0, 0)
            max_block(0, 0, 1)
            pe.wait_ge(s_wv, 32)
            for j in range(2):
                for h in range(4 * j, 4 * j + 4):
                    last = pe.matmul(PS[0:CD, j, DM * (h % 4):DM * (h % 4) + DM], wvT[:, h, :], wo_x[:, h, :],
                                     start=True, stop=True)
                last.then_inc(s_B_ps, 1)
            max_block(0, 0, 2)
            max_block(0, 0, 3)
            max_broadcast(0, 0)
            pe.wait_ge(s_qh, 2)
            pe.wait_ge(s_B, 2)

            for c in range(NCH):
                i, k = c // 2, c % 2
                for t in range(TPC):
                    n = TPC * c + t
                    score(k, c, t, n)
                    if t >= 1:
                        sum_values(i, k, c, t - 1, n - 1)
                    if c + 1 < NCH:
                        if 2 <= t <= 5:
                            max_block(1 - k, c + 1, t - 2)
                        if t == TPC - 1:
                            max_broadcast(1 - k, c + 1)
                sum_values(i, k, c, TPC - 1, TPC * c + TPC - 1)

            pe.wait_ge(s_cb, NCH)
            for h in range(XH):
                last = pe.matmul(PM[0:TOK, h // 4, (h // 2) % 2, 256 * (h % 2):256 * (h % 2) + DM + 1],
                                 acc[:, TOK * h:TOK * h + TOK], Bm[:, h, :], start=True, stop=True)
                if h % 2:
                    last.then_inc(s_y, 1)

            transpose_normed(2)
            pe.wait_ge(s_xnT, 2)
            pe.wait_ge(s_aw, 48)
            pe.matmul(PO[:, 0, 0:3 * DM], xnT[:, :], wqkv_sb[:, :], start=True, stop=True).then_inc(s_qkv, 1)
            pe.wait_ge(s_fb, 80)
            pe.wait_ge(s_x1, 1)
            for b in range(NB):
                pe.matmul(PM[:, b // 2, b % 2, :], b1_sb[:, b, :], sel_sb[:, :], start=True, stop=False,
                          skip_group_check=True)
            pe.wait_ge(s_qkn, 1)
            pe.transpose(PO[:, 1, 64:128], qkn[:, 0:DM], ident[0:TOK, 0:TOK])
            pe.transpose(PO[:, 1, 128:192], qkn[:, DM:2 * DM], ident[0:TOK, 0:TOK]).then_inc(s_qkT, 1)
            pe.wait_ge(s_qm, 1)
            pe.wait_ge(s_km, 2)
            pe.matmul(PS[:, 0, :], qm[:, :, :].rearrange("p a t -> p (a t)"),
                      km[:, :, :].rearrange("p g m -> p (g m)"), start=True, stop=True).then_inc(s_ss, 1)
            pe.wait_ge(s_sp, 1)
            for g in range(4):
                last = pe.transpose(PS[:, 1, 128 * g:128 * g + 128],
                                    pe_[:, 2 * g:2 * g + 2, :].rearrange("p g m -> p (g m)"), ident)
            last.then_inc(s_pt, 1)
            pe.matmul(PS[:, 0, 0:FC * TOK], b1_sb[0:FC, NB, :], sel_sb[0:FC, 0:FC * TOK], start=True, stop=False,
                      skip_group_check=True)
            pe.wait_ge(s_vm, 2)
            pe.wait_ge(s_ptc, 1)
            for g in range(4):
                last = pe.matmul(PO[:, 0, 34 * g:34 * g + 34], pT[:, g, :],
                                 vm[:, 2 * g:2 * g + 2, :].rearrange("p g e -> p (g e)"), start=True, stop=True)
            last.then_inc(s_so, 1)
            pe.wait_ge(s_ao, 2)
            pe.transpose(PO[0:DM // 2, 1, 192:320], ao[:, :, :].rearrange("p g e -> p (g e)"), ident).then_inc(s_aoT, 1)
            pe.wait_ge(s_aoTc, 1)
            for a in range(2):
                last = pe.matmul(PO[0:TOK, 0, 256:384], aoT[:, a, :], woT_sb[:, a, :], start=(a == 0), stop=(a == 1))
            last.then_inc(s_pj, 1)

            transpose_normed(3)
            pe.wait_ge(s_xnT, 3)
            pe.matmul(PO[0:TOK, 0, 384:384 + NE], xnT[:, 0:TOK], wg_sb[:, :], start=True, stop=True).then_inc(s_lg, 1)
            pe.wait_ge(s_fw1, 32)
            for b in [NB] + list(range(NB)):
                blocks = FC if b == NB else 8
                bank = PS[:, 0, :] if b == NB else PM[:, b // 2, b % 2, :]
                for j in range(blocks):
                    e = NE if b == NB else EPB * b + j // FC
                    last = pe.matmul(bank[:, TOK * j:TOK * j + TOK], w1_sb[:, e, 128 * (j % FC):128 * (j % FC) + 128],
                                     xnT[:, 0:TOK], start=False, stop=(j == blocks - 1), skip_group_check=True)
                last.then_inc(s_hid, 1)
            pe.wait_ge(s_cw, 1)
            pe.transpose(PO[0:NE + 1, 0, 0:TOK], cw[:, :], ident[0:TOK, 0:TOK]).then_inc(s_cwT, 1)
            pe.wait_ge(s_cwd, 1)
            pe.matmul(PS[:, 1, :], halves[:, :], cwd[:, :, :].rearrange("p e t -> p (e t)"),
                      start=True, stop=True).then_inc(s_cwb, 1)
            acc_y = PO[:, 1, 320:320 + TOK]
            pe.wait_ge(s_fw2, 32)
            pe.wait_ge(s_ws2, 1)
            pe.wait_ge(s_hs, 1)
            for f in range(FC):
                pe.matmul(acc_y, w2_sb[:, NE, f, :], hs[NB][:, TOK * f:TOK * f + TOK], start=(f == 0), stop=False)
            for b in range(NB):
                pe.wait_ge(s_hw, b + 1)
                for j in range(8):
                    last = pe.matmul(acc_y, w2_sb[:, EPB * b + j // FC, j % FC, :], hw[b][:, TOK * j:TOK * j + TOK],
                                     start=False, stop=(b == NB - 1 and j == 7))
            last.then_inc(s_yT, 1)
            pe.wait_ge(s_cwTc, 1)
            pe.matmul(PO[0:TOK, 0, 128:256], cwT[:, :], b2_sb[:, :], start=True, stop=False)
            pe.wait_ge(s_yTc, 1)
            pe.matmul(PO[0:TOK, 0, 128:256], yT[:, :], ident, start=False, stop=True).then_inc(s_yn, 1)


def _constants():
    import numpy as np
    c = np.zeros((128, C_W), np.float32)
    c[:, C_ID:C_ID + 128] = np.eye(128)
    r = np.arange(128)
    h = r // SD
    for g in range(8):
        c[:, C_MR + g] = h % 8 == g
        c[:, C_MV + g] = r // TOK == g % 2
    for a in range(2):
        c[:, C_ML + a] = h // 8 == a
    c[:, C_IO:C_IO + NE] = np.arange(NE)
    sel = np.repeat(np.eye(8, dtype=np.float32), TOK, axis=1)
    return c, sel


def kernel(**inputs):
    import numpy as np
    import concourse.bacc as bacc
    from concourse.bass_utils import run_bass_kernel_spmd

    g = {n.removeprefix("L0_"): np.asarray(a) for n, a in inputs.items()}
    ctx = g["ctx_768"][0].reshape(NCH, TILE, TPC, CD)
    v_cols = np.arange(DM).reshape(2, 8, SD).transpose(1, 0, 2).reshape(-1)
    consts, sel = _constants()
    arrays = {
        "x": g["x"][0],
        "ctx_n": ctx,
        "ctx_t": ctx.transpose(3, 0, 2, 1).reshape(CD, NCH, CHUNK),
        "wq_t": g["xattn_Wq"].reshape(DM, XH, XD).transpose(2, 1, 0),
        "wk_t": g["xattn_Wk"].reshape(CD, XH, XD).transpose(2, 1, 0),
        "wv_t": g["xattn_Wv"].reshape(CD, XH, XD).transpose(2, 1, 0),
        "wout": g["xattn_Wout"].reshape(XH, XD, DM).transpose(1, 0, 2),
        "bout": g["xattn_bout"],
        "wqkv": np.concatenate([g["attn_Wq"].T, g["attn_Wk"].T, g["attn_Wv"].T[:, v_cols]], axis=1),
        "wo_t": g["attn_Wo"].T.reshape(2, DM // 2, DM).transpose(1, 0, 2),
        "norm_w": np.stack([np.tile(g["attn_qn_w"], SH), np.tile(g["attn_kn_w"], SH)], axis=1),
        "wg": g["ffn_Wg"],
        "w1": g["ffn_W1"].transpose(1, 0, 2),
        "w2": g["ffn_W2"].reshape(NE, FC, 128, DM).transpose(2, 0, 1, 3),
        "ws1": g["ffn_Ws1"],
        "ws2": g["ffn_Ws2"].reshape(FC, 128, DM).transpose(1, 0, 2),
        "b1_rows": g["ffn_b1"].reshape(NB, 8, 128).transpose(1, 0, 2),
        "bs1_rows": g["ffn_bs1"].reshape(FC, 128),
        "b2_rows": np.concatenate([g["ffn_b2"], g["ffn_bs2"][None]], axis=0),
        "consts": consts,
        "sel8": sel,
    }
    nc = bacc.Bacc("TRN2", target_bir_lowering=False, num_devices=1)
    sent, aps = {}, []
    for name, a in arrays.items():
        a = np.ascontiguousarray(a)
        sent[f"in_{name}"] = a
        aps.append(nc.dram_tensor(f"in_{name}", a.shape, mybir.dt.from_np(a.dtype), kind="ExternalInput").ap())
    out = nc.dram_tensor("out", (TOK, DM), F32, kind="ExternalOutput").ap()
    build(nc, *aps, out)
    result = run_bass_kernel_spmd(nc, [sent], core_ids=[0])
    return result.results[0]["out"].reshape(1, TOK, DM)
```

```python
from contextlib import ExitStack

import concourse.bass as bass
from concourse import mybir

F32 = mybir.dt.float32
F32R = mybir.dt.float32r
BF16 = mybir.dt.bfloat16
U32 = mybir.dt.uint32
ALU = mybir.AluOpType
ACT = mybir.ActivationFunctionType
AX = mybir.AxisListType

TOK, DM = 64, 128
KEYS, CD = 6272, 96
XH, XD = 8, 128
Q = XH * TOK
QB = Q // 128
TILE = 128
TPC = 7
CHUNK = TPC * TILE
NCH = KEYS // CHUNK
SPANS = [(0,)] + [(c, c + 1) for c in range(1, NCH, 2)]
NSP = len(SPANS)
R32, RHI, RLO = 3, 4, 3
HALF = CHUNK // 2
XSCALE = 1.5 * XD ** -0.5
SH, SD = 16, 8
NE, FF = 8, 512
FC = FF // 128
EPB = 2
NB = NE // EPB
LN_EPS, RMS_EPS, W_EPS, SHARED = 1e-5, 1.1920928955078125e-07, 1e-9, 0.1
LOWEST = -3.0e38
WARM = 11

C_ID, C_MR, C_ML, C_MV, C_IO = 0, 128, 136, 138, 146
C_FO = 154
C_W = 218


def build(nc, x, ctx_n, ctx_t, wq_t, wk_t, wv_t, wout, bout, wqkv, wo_t, norm_w, wg, w1, w2, ws1, ws2,
          b1_rows, bs1_rows, b2_rows, consts, sel8, out):
    with ExitStack() as ctx:
        def sb(name, shape, dt=F32):
            return ctx.enter_context(nc.sbuf_tensor(name, shape, dt))

        def pb(name, shape, dt=F32):
            return ctx.enter_context(nc.psum_tensor(name, shape, dt))

        def sem(name):
            return ctx.enter_context(nc.semaphore(name))

        x_sb = sb("x_sb", [TOK, DM])
        xb = sb("xb", [2 * TOK, DM])
        warm = sb("warm", [128, 512], BF16)
        bout_b = sb("bout_b", [TOK, DM])
        cst = sb("cst", [128, C_W])
        ident_r = sb("ident_r", [128, 128], F32R)
        expo = sb("expo", [TOK, 1])
        wqT = sb("wqT", [128, XH, DM])
        wkT = sb("wkT", [128, XH, CD])
        wvT = sb("wvT", [128, XH, CD])
        wo_x = sb("wo_x", [128, XH, DM])
        A = sb("A", [128, XH, CD])
        Bm = sb("Bm", [CD + 1, XH, DM + 1])
        ctx32 = [sb(f"ctx32_{p}", [CD, CHUNK]) for p in range(R32)]
        ctx_hi = [sb(f"ctx_hi_{p}", [CD + 1, CHUNK], F32R) for p in range(RHI)]
        ctx_lo = [sb(f"ctx_lo_{p}", [CD, CHUNK], F32R) for p in range(RLO)]
        val32 = [sb(f"val32_{p}", [128, TPC, CD + 1]) for p in range(2)]
        val_hi = [sb(f"val_hi_{p}", [128, TPC, CD + 1], F32R) for p in range(2)]
        val_lo = [sb(f"val_lo_{p}", [128, TPC, CD + 1], F32R) for p in range(2)]
        q_hi = [sb(f"q_hi_{p}", [CD + 1, Q], F32R) for p in range(2)]
        q_lo = sb("q_lo", [CD, Q], F32R)
        mx = [sb(f"mx_{p}", [128, QB]) for p in range(2)]
        m_run = [sb(f"m_run_{p}", [128, QB], F32R) for p in range(2)]
        m_row = [sb(f"m_row_{p}", [CD + 1, Q]) for p in range(2)]
        m_diff = sb("m_diff", [CD + 1, Q])
        alpha = sb("alpha", [CD + 1, Q])
        p_hi = [sb(f"p_hi_{i}", [128, Q], F32R) for i in range(3)]
        p_lo = [sb(f"p_lo_{i}", [128, Q], F32R) for i in range(3)]
        p32 = [sb(f"p32_{i}", [128, Q]) for i in range(2)]
        acc = sb("acc", [CD + 1, Q])
        st = sb("st", [TOK, 6])
        mv = sb("mv", [TOK, 2])
        ve = sb("ve", [TOK, 1])
        rstd = sb("rstd", [TOK, 1])
        xn = sb("xn", [TOK, DM])
        xnT = sb("xnT", [DM, 2 * TOK])
        xr = [sb(f"xr_{i}", [2 * TOK, DM]) for i in range(4)]
        x1 = sb("x1", [TOK, DM])
        rs_x = sb("rs_x", [2 * TOK, XH // 2])
        wqkv_sb = sb("wqkv_sb", [DM, 3 * DM])
        woT_sb = sb("woT_sb", [DM // 2, 2, DM])
        nw = sb("nw", [128, 2])
        wn = sb("wn", [128, 1])
        wmask = sb("wmask", [128, 2])
        sq = sb("sq", [TOK, 2 * DM])
        ms = sb("ms", [TOK, 2 * SH])
        mse = sb("mse", [TOK, 2 * SH])
        rr = sb("rr", [TOK, 2 * SH])
        qkn = sb("qkn", [TOK, 2 * DM])
        qm = sb("qm", [128, 2, TOK])
        km = sb("km", [128, 8, TOK])
        vm = sb("vm", [128, 8, 17])
        smax = sb("smax", [128, 8])
        sd = sb("sd", [128, 8, TOK])
        pe_ = sb("pe_", [128, 8, TOK])
        pT = sb("pT", [128, 4, 128])
        rsum = sb("rsum", [128, 8])
        ao = sb("ao", [128, 8, 8])
        aoT = sb("aoT", [DM // 2, 2, TOK])
        x2 = sb("x2", [TOK, DM])
        wg_sb = sb("wg_sb", [DM, NE])
        w1_sb = sb("w1_sb", [DM, NE + 1, FF])
        w2_sb = sb("w2_sb", [128, NE + 1, FC, DM])
        b1_sb = sb("b1_sb", [8, NB + 1, 128])
        b2_sb = sb("b2_sb", [NE + 1, DM])
        sel_sb = sb("sel_sb", [8, 8 * TOK])
        halves = sb("halves", [TOK, 128])
        nlm = sb("nlm", [TOK, 1])
        le = sb("le", [TOK, NE])
        ls = sb("ls", [TOK, 1])
        lr = sb("lr", [TOK, 1])
        pr = sb("pr", [TOK, NE])
        v8 = sb("v8", [TOK, 8])
        i8 = sb("i8", [TOK, 8], U32)
        if8 = sb("if8", [TOK, 2])
        wsum = sb("wsum", [TOK, 1])
        wr = sb("wr", [TOK, 1])
        w2v = sb("w2v", [TOK, 2])
        c1 = sb("c1", [TOK, NE])
        c2 = sb("c2", [TOK, NE])
        cw = sb("cw", [TOK, NE + 1])
        cwd = sb("cwd", [TOK, NE, TOK])
        dummy = sb("table_dummy", [1, 2])
        rroot = sb("rroot", [TOK, 2 * SH])
        cwT = sb("cwT", [NE + 1, TOK])
        th = [sb(f"th_{b}", [128, 8 * TOK]) for b in range(NB + 1)]
        hs = [sb(f"hs_{b}", [128, 8 * TOK]) for b in range(NB + 1)]
        hw = [sb(f"hw_{b}", [128, 8 * TOK]) for b in range(NB)]
        y = sb("y", [TOK, DM])

        PM = pb("PM", [128, 2, 2, 512])
        PS = pb("PS", [128, 2, 512])
        PO = pb("PO", [128, 2, 512])

        s_x = sem("x_loaded")
        s_cst = sem("consts_loaded")
        s_bout = sem("bout_loaded")
        s_wq = sem("wq_loaded")
        s_wk = sem("wk_loaded")
        s_wv = sem("wv_wout_loaded")
        s_aw = sem("attn_weights_loaded")
        s_fw1 = sem("w1_loaded")
        s_fw2 = sem("w2_loaded")
        s_fb = sem("ffn_small_loaded")
        s_ct = [sem(f"ctx32_{p}_loaded") for p in range(R32)]
        s_cv = [sem(f"val_{p}_loaded") for p in range(2)]
        s_ones = sem("constants_set")
        s_dz = sem("vector_constants_set")
        s_idr = sem("ident_rounded")
        s_ve = sem("variance_ready")
        s_pow = sem("inverse_root_ready")
        s_xn = sem("normed_ready")
        s_xnT_ps = sem("normed_transposed")
        s_xnT = sem("normed_T_ready")
        s_A_ps = sem("A_in_psum")
        s_A = sem("A_ready")
        s_B_ps = sem("B_in_psum")
        s_B = sem("B_ready")
        s_q_ps = sem("queries_in_psum")
        s_qh = sem("q_hi_ready")
        s_ql = sem("q_lo_ready")
        s_hi = sem("ctx_hi_ready")
        s_lo = sem("ctx_lo_ready")
        s_mm = sem("max_scores_ready")
        s_mr = sem("max_reduced")
        s_bc = sem("max_broadcast_ready")
        s_row = sem("shift_row_ready")
        s_mb = sem("max_row_copied")
        s_mc = sem("chunk_max_ready")
        s_df = sem("max_diff_ready")
        s_al = sem("alpha_ready")
        s_sc = sem("scores_ready")
        s_eh = sem("probs_hi_ready")
        s_ex = sem("probs_ready")
        s_pl = sem("probs_lo_ready")
        s_vh = sem("val_hi_ready")
        s_vl = sem("val_lo_ready")
        s_wz = sem("warm_set")
        s_fold = sem("heads_scaled")
        s_x1p = sem("x1_in_psum")
        s_rt = sem("roots_ready")
        s_dm = sem("dummy_done")
        s_pv = sem("tile_summed")
        s_am = sem("acc_scaled")
        s_cb = sem("span_combined")
        s_y = sem("heads_projected")
        s_x1 = sem("x1_copied")
        s_dve = sem("vector_step")
        s_qkv = sem("qkv_in_psum")
        s_sq = sem("squares_ready")
        s_mse = sem("mean_squares_ready")
        s_qkn = sem("qk_normed")
        s_qkT = sem("qk_transposed")
        s_qm = sem("q_masked")
        s_km = sem("k_masked")
        s_vm = sem("v_masked")
        s_ss = sem("self_scores_ready")
        s_sd = sem("self_scores_shifted")
        s_sp = sem("self_probs_ready")
        s_pt = sem("self_probs_transposed")
        s_ptc = sem("self_probs_T_ready")
        s_so = sem("self_sums_ready")
        s_ao = sem("self_out_ready")
        s_aoT = sem("self_out_transposed")
        s_aoTc = sem("self_out_T_ready")
        s_pj = sem("self_projected")
        s_x2 = sem("x2_ready")
        s_lg = sem("logits_ready")
        s_nl = sem("logit_max_ready")
        s_le = sem("logit_exp_ready")
        s_cw = sem("gates_ready")
        s_cwT = sem("gates_transposed")
        s_cwTc = sem("gates_T_ready")
        s_cwd = sem("gates_diagonal_ready")
        s_cwb = sem("gates_broadcast")
        s_ws2 = sem("ws2_scaled")
        s_hid = sem("hidden_ready")
        s_th = sem("tanh_ready")
        s_hs = sem("silu_ready")
        s_hw = sem("weighted_ready")
        s_yn = sem("y_in_psum")
        s_fin = sem("result_ready")
        s_out = sem("result_stored")

        ident = cst[:, C_ID:C_ID + 128]
        block = ctx.enter_context(nc.Block())

        max_blocks, broadcast_after = {}, {}
        for s, span in enumerate(SPANS[:-1]):
            after = SPANS[s + 1]
            todo = [(c, b) for c in after for b in range(QB)]
            slots = [(span[0], t) for t in (0, 1, 2, 3, 3, 4, 5, 5)] if len(span) == 1 else \
                [(span[0], t) for t in (1, 2, 3, 4)] + [(span[1], t) for t in (0, 1, 2, 3)]
            for slot, item in zip(slots, todo):
                max_blocks.setdefault(slot, []).append(item)
            broadcast_after[(span[-1], TPC - 1 if len(span) == 1 else TPC - 2)] = s + 1
        span_of = {c: s for s, span in enumerate(SPANS) for c in span}
        tiles_before = [TPC * span[0] for span in SPANS] + [TPC * NCH]

        @block.sync
        def _(sp):
            sp.dma_start(x_sb[:, :], x).then_inc(s_x, 16)
            sp.dma_start(wkT[:, :, :], wk_t).then_inc(s_wk, 16)
            sp.dma_start(ctx32[0][:, :], ctx_t[:, 0, :]).then_inc(s_ct[0], 16)
            sp.dma_start(bout_b[:, :], bout.rearrange("(a n) -> a n", a=1).to_broadcast([TOK, DM])).then_inc(s_bout, 16)
            sp.dma_start(wvT[:, :, :], wv_t).then_inc(s_wv, 16)
            sp.dma_start(wo_x[:, :, :], wout).then_inc(s_wv, 16)
            sp.dma_start(val32[0][:, :, 0:CD], ctx_n[0]).then_inc(s_cv[0], 16)
            sp.dma_start(ctx32[1][:, :], ctx_t[:, 1, :]).then_inc(s_ct[1], 16)
            sp.dma_start(ctx32[2][:, :], ctx_t[:, 2, :]).then_inc(s_ct[2], 16)
            sp.dma_start(val32[1][:, :, 0:CD], ctx_n[1]).then_inc(s_cv[1], 16)
            sp.dma_start(wqkv_sb[:, :], wqkv).then_inc(s_aw, 16)
            sp.dma_start(woT_sb[:, :, :], wo_t).then_inc(s_aw, 16)
            sp.dma_start(nw[:, :], norm_w).then_inc(s_aw, 16)
            sp.dma_start(wg_sb[:, :], wg).then_inc(s_fb, 16)
            sp.dma_start(b1_sb[:, 0:NB, :], b1_rows).then_inc(s_fb, 16)
            sp.dma_start(b1_sb[0:FC, NB, :], bs1_rows).then_inc(s_fb, 16)
            sp.dma_start(b2_sb[:, :], b2_rows).then_inc(s_fb, 16)
            sp.dma_start(sel_sb[:, :], sel8).then_inc(s_fb, 16)
            sp.dma_start(w2_sb[:, NE, :, :], ws2).then_inc(s_fw2, 16)

            def load_ctx(c):
                sp.wait_ge(s_hi, c - R32 + 1)
                sp.wait_ge(s_lo, c - R32 + 1)
                sp.dma_start(ctx32[c % R32][:, :], ctx_t[:, c, :]).then_inc(s_ct[c % R32], 16)

            def load_val(c):
                sp.wait_ge(s_vh, c - 1)
                sp.wait_ge(s_vl, c - 1)
                sp.dma_start(val32[c % 2][:, :, 0:CD], ctx_n[c]).then_inc(s_cv[c % 2], 16)

            load_ctx(3)
            load_val(2)
            sp.dma_start(w1_sb[:, 0:NE, :], w1).then_inc(s_fw1, 16)
            sp.dma_start(w1_sb[:, NE, :], ws1).then_inc(s_fw1, 16)
            sp.dma_start(w2_sb[:, 0:NE, :, :], w2).then_inc(s_fw2, 16)
            for c in range(3, NCH):
                if c + 1 < NCH:
                    load_ctx(c + 1)
                load_val(c)
            sp.wait_ge(s_fin, 1)
            sp.dma_start(out, y[:, :]).then_inc(s_out, 16)
            sp.wait_ge(s_out, 16)

        @block.gpsimd
        def _(pool):
            fills = [(expo[:, :], -0.5), (Bm[:, :, :], 0.0), (Bm[CD:CD + 1, :, DM:DM + 1], 1.0), (halves[:, :], 0.5),
                     (cw[:, NE:NE + 1], SHARED), (vm[:, :, 16:17], 0.0)]
            fills += [(ctx_hi[p][CD:CD + 1, :].bitcast(F32), 1.0) for p in range(RHI)]
            fills += [(val32[p][:, :, CD:CD + 1], 1.0) for p in range(2)]
            for n, (place, value) in enumerate(fills):
                pool.memset(place, value).then_inc(s_ones, 1)
                pool.wait_ge(s_ones, n + 1)

            def inverse_root(n):
                pool.wait_ge(s_ve, n)
                pool.tensor_tensor(rstd[:, :], ve[:, :], expo[:, :], ALU.pow).then_inc(s_pow, 1)

            def low_part(c):
                pool.wait_ge(s_hi, c + 1)
                if c >= RLO:
                    pool.wait_ge(s_sc, TPC * (c - RLO + 1))
                pool.tensor_tensor(ctx_lo[c % RLO][:, :], ctx32[c % R32][:, :],
                                   ctx_hi[c % RHI][0:CD, :].bitcast(F32), ALU.subtract).then_inc(s_lo, 1)

            def low_values(c):
                pool.wait_ge(s_vh, c + 1)
                if c >= 2:
                    pool.wait_ge(s_pv, TPC * (c - 1))
                pool.tensor_tensor(val_lo[c % 2][:, :, :], val32[c % 2][:, :, :],
                                   val_hi[c % 2][:, :, :].bitcast(F32), ALU.subtract).then_inc(s_vl, 1)

            def max_change(s):
                pool.wait_ge(s_mb, s + 1)
                if s == 0:
                    pool.wait_ge(s_dz, 3)
                if s >= 1:
                    pool.wait_ge(s_al, s)
                pool.tensor_tensor(m_diff[:, :], m_row[1 - s % 2][:, :], m_row[s % 2][:, :],
                                   ALU.subtract).then_inc(s_df, 1)

            inverse_root(1)
            low_part(0)
            low_values(0)
            low_part(1)
            max_change(0)
            low_part(2)
            for c in range(NCH):
                if c + 1 < NCH:
                    low_values(c + 1)
                if c + 3 < NCH:
                    low_part(c + 3)
                if c == SPANS[span_of[c]][-1] and span_of[c] + 1 < NSP:
                    max_change(span_of[c] + 1)
            inverse_root(2)
            inverse_root(3)

        @block.scalar
        def _(act):
            act.dma_start(wqT[:, :, :], wq_t).then_inc(s_wq, 16)
            act.dma_start(cst[:, :], consts).then_inc(s_cst, 16)
            def high_values(c):
                act.wait_ge(s_cv[c % 2], 16 * (c // 2 + 1))
                if c >= 2:
                    act.wait_ge(s_pv, TPC * (c - 1))
                act.activation(val_hi[c % 2][:, :, :], val32[c % 2][:, :, :], ACT.Copy).then_inc(s_vh, 1)

            for j in range(2):
                act.wait_ge(s_A_ps, j + 1)
                act.activation(A[:, 4 * j:4 * j + 4, :], PS[:, j, 0:4 * CD].rearrange("p (h c) -> p h c", h=4),
                               ACT.Copy, scale=XSCALE).then_inc(s_A, 1)
            act.wait_ge(s_q_ps, 1)
            act.activation(q_hi[0][0:CD, :], PO[0:CD, 0, :], ACT.Copy).then_inc(s_qh, 1)
            act.wait_ge(s_qh, 1)
            act.activation(q_hi[1][0:CD, :], q_hi[0][0:CD, :].bitcast(F32), ACT.Copy).then_inc(s_qh, 1)
            act.wait_ge(s_ones, 6 + RHI + 2)
            high_values(0)
            for j in range(2):
                act.wait_ge(s_B_ps, j + 1)
                act.activation(Bm[0:CD, 4 * j:4 * j + 4, 0:DM], PS[0:CD, j, :].rearrange("p (h c) -> p h c", h=4),
                               ACT.Copy).then_inc(s_B, 1)

            def max_rows(s):
                act.wait_ge(s_bc, s + 1)
                if s >= 2:
                    act.wait_ge(s_sc, tiles_before[s - 1])
                    act.wait_ge(s_df, s)
                act.activation(q_hi[s % 2][CD:CD + 1, :], PM[CD:CD + 1, 0, 0, :], ACT.Copy, scale=-1.0).then_inc(s_row, 1)
                act.activation(m_row[s % 2][:, :], PM[0:CD + 1, 0, 0, :], ACT.Copy).then_inc(s_mb, 1)

            max_rows(0)
            for c in range(NCH):
                s = span_of[c]
                for t in range(TPC):
                    n = TPC * c + t
                    act.wait_ge(s_sc, n + 1)
                    if n >= 3:
                        act.wait_ge(s_pv, n - 2)
                    act.activation(p_hi[n % 3][:, :], PS[:, n % 2, :], ACT.Exp).then_inc(s_eh, 1)
                    if n >= 2:
                        act.wait_ge(s_pl, n - 1)
                    act.activation(p32[n % 2][:, :], PS[:, n % 2, :], ACT.Exp).then_inc(s_ex, 1)
                    if t == 2 and c + 1 < NCH:
                        high_values(c + 1)
                    if t == 3 and c == SPANS[s][0]:
                        act.wait_ge(s_df, s + 1)
                        if s >= 1:
                            act.wait_ge(s_am, s)
                        act.activation(alpha[:, :], m_diff[:, :], ACT.Exp).then_inc(s_al, 1)
                if c == SPANS[s][-1] and s + 1 < NSP:
                    max_rows(s + 1)

            act.wait_ge(s_fw2, 32)
            act.activation(w2_sb[:, NE, :, :], w2_sb[:, NE, :, :], ACT.Copy, scale=0.5 * SHARED).then_inc(s_ws2, 1)
            act.activation(dummy[:, 0:1], cst[0:1, 0:1], ACT.Sqrt).then_inc(s_dm, 1)
            act.wait_ge(s_qkv, 1)
            act.activation(sq[:, :], PO[0:TOK, 0, 0:2 * DM], ACT.Square).then_inc(s_sq, 1)
            act.wait_ge(s_mse, 1)
            act.activation(rroot[:, :], mse[:, :], ACT.Sqrt).then_inc(s_rt, 1)
            act.activation(dummy[:, 1:2], cst[0:1, 0:1], ACT.Exp).then_inc(s_dm, 1)
            act.wait_ge(s_sd, 1)
            act.activation(pe_[:, :, :], sd[:, :, :], ACT.Exp).then_inc(s_sp, 1)
            act.wait_ge(s_nl, 1)
            act.activation(le[:, :], PO[0:TOK, 0, 384:384 + NE], ACT.Exp, bias=nlm[:, 0:1],
                           accum_out=ls[:, :]).then_inc(s_le, 1)
            for n, b in enumerate([NB] + list(range(NB))):
                w = FC * TOK if b == NB else 8 * TOK
                src = PS[:, 0, 0:w] if b == NB else PM[:, b // 2, b % 2, :]
                act.wait_ge(s_hid, n + 1)
                act.activation(th[b][:, 0:w], src, ACT.Tanh, scale=0.5).then_inc(s_th, 1)

        @block.vector
        def _(dve):
            steps = [0]

            def link(ins):
                steps[0] += 1
                ins.then_inc(s_dve, 1)
                dve.wait_ge(s_dve, steps[0])

            def layer_norm(n, src, copies):
                link(dve.bn_stats(st[:, :], src))
                link(dve.bn_aggr(mv[:, :], st[:, :]))
                dve.tensor_scalar(ve[:, :], mv[:, 1:2], LN_EPS, None, ALU.add).then_inc(s_ve, 1)
                dve.wait_ge(s_pow, n)
                dve.tensor_scalar(xn[:, :], src, mv[:, 0:1], rstd[:, 0:1], ALU.subtract,
                                  ALU.mult).then_inc(s_xn, 1)
                dve.wait_ge(s_xnT_ps, n)
                if copies == 2:
                    dve.tensor_copy(xnT[:, :].rearrange("p (a t) -> p a t", a=2),
                                    PO[:, 1, None, 0:TOK].to_broadcast([128, 2, TOK])).then_inc(s_xnT, 1)
                else:
                    dve.tensor_copy(xnT[:, 0:TOK], PO[:, 1, 0:TOK]).then_inc(s_xnT, 1)

            dve.memset(warm[:, :], 0.0).then_inc(s_wz, 1)
            dve.memset(m_run[1][:, :].bitcast(F32), LOWEST).then_inc(s_dz, 1)
            dve.memset(m_row[1][:, :], LOWEST).then_inc(s_dz, 1)
            dve.memset(acc[:, :], 0.0).then_inc(s_dz, 1)
            dve.memset(xb[TOK:2 * TOK, :], 0.0).then_inc(s_dz, 1)
            dve.wait_ge(s_x, 16)
            layer_norm(1, x_sb[:, :], 1)

            def high_part(c):
                dve.wait_ge(s_ct[c % R32], 16 * (c // R32 + 1))
                if c >= RHI:
                    dve.wait_ge(s_sc, TPC * (c - RHI + 1))
                dve.tensor_copy(ctx_hi[c % RHI][0:CD, :], ctx32[c % R32][:, :]).then_inc(s_hi, 1)

            def reduce_block(c, b):
                dve.wait_ge(s_mm, QB * c + b + 1)
                if b == 0 and c >= 2:
                    dve.wait_ge(s_mc, c - 1)
                dve.tensor_reduce(mx[c % 2][:, b:b + 1], PM[:, b % 2, :, 0:HALF], AX.XY, ALU.max).then_inc(s_mr, 1)

            def running_max(c):
                dve.wait_ge(s_mr, QB * (c + 1))
                if c >= 1:
                    dve.wait_ge(s_mc, c)
                if c >= 2:
                    dve.wait_ge(s_bc, sum(span[-1] <= c - 2 for span in SPANS))
                dve.tensor_tensor(m_run[c % 2][:, :], mx[c % 2][:, :], m_run[1 - c % 2][:, :].bitcast(F32),
                                  ALU.max).then_inc(s_mc, 1)

            def low_probs(n):
                dve.wait_ge(s_ex, n + 1)
                if n >= 3:
                    dve.wait_ge(s_pv, n - 2)
                dve.tensor_tensor(p_lo[n % 3][:, :], p32[n % 2][:, :], p_hi[n % 3][:, :].bitcast(F32),
                                  ALU.subtract).then_inc(s_pl, 1)

            def scale_sums(s):
                dve.wait_ge(s_al, s + 1)
                if s >= 1:
                    dve.wait_ge(s_cb, s)
                dve.tensor_tensor(acc[:, :], acc[:, :], alpha[:, :], ALU.mult).then_inc(s_am, 1)

            def add_sums(s):
                dve.wait_ge(s_am, s + 1)
                dve.wait_ge(s_pv, tiles_before[s + 1])
                dve.tensor_tensor(acc[:, :], acc[:, :], PO[0:CD + 1, s % 2, :], ALU.add).then_inc(s_cb, 1)

            dve.wait_ge(s_cst, 16)
            dve.tensor_copy(ident_r[:, :], ident).then_inc(s_idr, 1)
            high_part(0)
            dve.wait_ge(s_dz, 4)
            dve.wait_ge(s_qh, 1)
            dve.tensor_tensor(q_lo[:, :], PO[0:CD, 0, :], q_hi[0][0:CD, :].bitcast(F32), ALU.subtract).then_inc(s_ql, 1)
            for b in range(QB):
                reduce_block(0, b)
                if b == 1:
                    high_part(1)
            running_max(0)
            high_part(2)
            for c in range(NCH):
                s = span_of[c]
                for t in range(TPC):
                    low_probs(TPC * c + t)
                    if t == 0 and c + 3 < NCH:
                        high_part(c + 3)
                    if c == SPANS[s][0]:
                        if t == 2 and s >= 1:
                            add_sums(s - 1)
                        if t == 5:
                            scale_sums(s)
                    for item in max_blocks.get((c, t), []):
                        reduce_block(*item)
                        if item[1] == QB - 1:
                            running_max(item[0])
                if c == 1:
                    dve.wait_ge(s_bout, 16)
                    dve.tensor_tensor(xb[0:TOK, :], x_sb[:, :], bout_b[:, :], ALU.add).then_inc(s_dz, 1)
                    dve.wait_ge(s_aw, 48)
                    link(dve.tensor_tensor(wn[:, :], nw[:, 0:1], nw[:, 1:2], ALU.mult))
                    link(dve.tensor_scalar(wmask[:, :], cst[:, C_ML:C_ML + 2], wn[:, 0:1], SD ** -0.5, ALU.mult,
                                           ALU.mult))
            add_sums(NSP - 1)

            dve.wait_ge(s_dz, 5)
            src = xb
            for g in range(XH // 2):
                Y = PM[:, g // 2, g % 2, 0:DM + 1]
                dve.wait_ge(s_y, g + 1)
                link(dve.reciprocal(rs_x[:, g:g + 1], Y[:, DM:DM + 1]))
                ins = dve.scalar_tensor_tensor(out=xr[g][:, :], in0=Y[:, 0:DM], scalar=rs_x[:, g:g + 1], in1=src[:, :],
                                               op0=ALU.mult, op1=ALU.add)
                if g == XH // 2 - 1:
                    ins.then_inc(s_fold, 1)
                else:
                    link(ins)
                src = xr[g]
            dve.wait_ge(s_x1p, 1)

            x1_ps = PS[0:TOK, 1, 0:DM]
            layer_norm(2, x1_ps, 2)
            dve.tensor_copy(x1[:, :], x1_ps).then_inc(s_x1, 1)
            dve.wait_ge(s_sq, 1)
            link(dve.tensor_reduce(ms[:, :], sq[:, :].rearrange("p (g d) -> p g d", d=SD), AX.X, ALU.add))
            dve.tensor_scalar(mse[:, :], ms[:, :], 1.0 / SD, RMS_EPS, ALU.mult, ALU.add).then_inc(s_mse, 1)
            dve.wait_ge(s_ones, 6 + RHI + 2)
            dve.tensor_tensor(vm[:, :, 0:16], PO[:, 0, 2 * DM:3 * DM].rearrange("p (g e) -> p g e", e=16),
                              cst[:, C_MV:C_MV + 8, None].to_broadcast([128, 8, 16]), ALU.mult).then_inc(s_vm, 1)
            dve.tensor_copy(vm[:, :, 16], cst[:, C_MV:C_MV + 8]).then_inc(s_vm, 1)
            dve.wait_ge(s_rt, 1)
            link(dve.reciprocal(rr[:, :], rroot[:, :]))
            dve.tensor_tensor(qkn[:, :].rearrange("p (g d) -> p g d", d=SD),
                              PO[0:TOK, 0, 0:2 * DM].rearrange("p (g d) -> p g d", d=SD),
                              rr[:, :, None].to_broadcast([TOK, 2 * SH, SD]), ALU.mult).then_inc(s_qkn, 1)
            dve.wait_ge(s_qkT, 1)
            dve.tensor_tensor(qm[:, :, :], PO[:, 1, None, 64:128].to_broadcast([128, 2, TOK]),
                              wmask[:, :, None].to_broadcast([128, 2, TOK]), ALU.mult).then_inc(s_qm, 1)
            for j in range(2):
                dve.tensor_tensor(km[:, 4 * j:4 * j + 4, :], PO[:, 1, None, 128:192].to_broadcast([128, 4, TOK]),
                                  cst[:, C_MR + 4 * j:C_MR + 4 * j + 4, None].to_broadcast([128, 4, TOK]),
                                  ALU.mult).then_inc(s_km, 1)
            dve.wait_ge(s_ss, 1)
            S = PS[:, 0, :].rearrange("p (g m) -> p g m", g=8)
            link(dve.tensor_reduce(smax[:, :], S, AX.X, ALU.max))
            dve.tensor_tensor(sd[:, :, :], S, smax[:, :, None].to_broadcast([128, 8, TOK]), ALU.subtract).then_inc(s_sd, 1)
            dve.wait_ge(s_pt, 1)
            dve.tensor_copy(pT[:, :, :], PS[:, 1, :].rearrange("p (g m) -> p g m", g=4)).then_inc(s_ptc, 1)
            dve.wait_ge(s_so, 1)
            O = PO[:, 0, 0:8 * 17].rearrange("p (g e) -> p g e", e=17)
            link(dve.reciprocal(rsum[:, :], O[:, :, 16]))
            for a in range(2):
                rows = slice(TOK * a, TOK * a + TOK)
                dve.tensor_tensor(ao[rows, :, :], O[rows, :, SD * a:SD * a + SD],
                                  rsum[rows, :, None].to_broadcast([TOK, 8, SD]), ALU.mult).then_inc(s_ao, 1)
            dve.wait_ge(s_aoT, 1)
            dve.tensor_copy(aoT[:, :, :], PO[0:DM // 2, 1, 192:320].rearrange("p (a t) -> p a t", a=2)).then_inc(s_aoTc, 1)
            dve.wait_ge(s_x1, 1)
            dve.wait_ge(s_pj, 1)
            dve.tensor_tensor(x2[:, :], x1[:, :], PO[0:TOK, 0, 256:384], ALU.add).then_inc(s_x2, 1)
            dve.wait_ge(s_x2, 1)

            layer_norm(3, x2[:, :], 1)
            dve.wait_ge(s_lg, 1)
            dve.tensor_reduce(nlm[:, :], PO[0:TOK, 0, 384:384 + NE], AX.X, ALU.max, negate=True).then_inc(s_nl, 1)
            dve.wait_ge(s_le, 1)
            link(dve.reciprocal(lr[:, :], ls[:, :]))
            link(dve.tensor_scalar(pr[:, :], le[:, :], lr[:, 0:1], None, ALU.mult))
            link(dve.max(v8[:, :], pr[:, :]))
            dve.max_index(i8[:, :], v8[:, :], pr[:, :]).then_inc(s_dve, 1)
            steps[0] += 1
            link(dve.tensor_scalar(wsum[:, :], v8[:, 0:1], v8[:, 1:2], W_EPS, ALU.add, ALU.add))
            link(dve.reciprocal(wr[:, :], wsum[:, :]))
            dve.tensor_copy(if8[:, :], i8[:, 0:2]).then_inc(s_dve, 1)
            steps[0] += 1
            link(dve.tensor_scalar(w2v[:, :], v8[:, 0:2], wr[:, 0:1], None, ALU.mult))
            dve.tensor_scalar(c1[:, :], cst[0:TOK, C_IO:C_IO + NE], if8[:, 0:1], w2v[:, 0:1], ALU.is_equal,
                              ALU.mult).then_inc(s_dve, 1)
            steps[0] += 1
            link(dve.tensor_scalar(c2[:, :], cst[0:TOK, C_IO:C_IO + NE], if8[:, 1:2], w2v[:, 1:2], ALU.is_equal,
                                   ALU.mult))
            dve.tensor_tensor(cw[:, 0:NE], c1[:, :], c2[:, :], ALU.add).then_inc(s_cw, 1)
            dve.wait_ge(s_cw, 1)
            dve.tensor_tensor(cwd[:, :, :], cst[0:TOK, None, C_ID:C_ID + TOK].to_broadcast([TOK, NE, TOK]),
                              cw[:, 0:NE, None].to_broadcast([TOK, NE, TOK]), ALU.mult).then_inc(s_cwd, 1)

            def silu(n, b, w, src):
                dve.wait_ge(s_th, n + 1)
                dve.scalar_tensor_tensor(out=hs[b][:, 0:w], in0=th[b][:, 0:w], scalar=1.0, in1=src,
                                         op0=ALU.add, op1=ALU.mult).then_inc(s_hs, 1)

            silu(0, NB, FC * TOK, PS[:, 0, 0:FC * TOK])
            dve.wait_ge(s_cwT, 1)
            dve.tensor_copy(cwT[:, :], PO[0:NE + 1, 0, 0:TOK]).then_inc(s_cwTc, 1)
            for b in range(NB):
                silu(b + 1, b, 8 * TOK, PM[:, b // 2, b % 2, :])
                dve.wait_ge(s_hs, b + 2)
                dve.wait_ge(s_cwb, 1)
                cwb = PS[:, 1, :].rearrange("p (e t) -> p e t", e=NE)[:, EPB * b:EPB * b + EPB, None, :]
                dve.tensor_tensor(hw[b][:, :].rearrange("p (e f t) -> p e f t", e=EPB, f=FC),
                                  hs[b][:, :].rearrange("p (e f t) -> p e f t", e=EPB, f=FC),
                                  cwb.to_broadcast([128, EPB, FC, TOK]), ALU.mult).then_inc(s_hw, 1)
            dve.wait_ge(s_yn, 1)
            dve.tensor_tensor(y[:, :], x2[:, :], PO[0:TOK, 1, 320:320 + DM], ALU.add).then_inc(s_fin, 1)

        @block.tensor
        def _(pe):
            def transpose_normed(n):
                pe.wait_ge(s_xn, n)
                pe.transpose(PO[:, 1, 0:TOK], xn[:, :], ident[0:TOK, 0:TOK]).then_inc(s_xnT_ps, 1)

            pe.wait_ge(s_wz, 1)
            for _ in range(WARM):
                pe.matmul(PM[:, 0, 0, :], warm[:, 0:128], warm[:, :], start=True, stop=True)
            pe.wait_ge(s_wq, 16)
            pe.wait_ge(s_wk, 16)
            for j in range(2):
                for h in range(4 * j, 4 * j + 4):
                    last = pe.matmul(PS[:, j, CD * (h % 4):CD * (h % 4) + CD], wqT[:, h, :], wkT[:, h, :],
                                     start=True, stop=True)
                last.then_inc(s_A_ps, 1)
            pe.wait_ge(s_cst, 16)
            transpose_normed(1)
            pe.wait_ge(s_xnT, 1)
            for h in range(XH):
                if h % 4 == 0:
                    pe.wait_ge(s_A, h // 4 + 1)
                last = pe.matmul(PO[0:CD, 0, TOK * h:TOK * h + TOK], A[:, h, :], xnT[:, 0:TOK], start=True, stop=True)
            last.then_inc(s_q_ps, 1)

            def max_block(c, b):
                if b == 0:
                    pe.wait_ge(s_hi, c + 1)
                    if c >= 1:
                        read = sum(span[-1] < c for span in SPANS)
                        pe.wait_ge(s_row, read)
                        pe.wait_ge(s_mb, read)
                if QB * c + b >= 2:
                    pe.wait_ge(s_mr, QB * c + b - 1)
                for j in range(2):
                    last = pe.matmul(PM[:, b % 2, j, 0:HALF], q_hi[0][0:CD, 128 * b:128 * b + 128],
                                     ctx_hi[c % RHI][0:CD, HALF * j:HALF * j + HALF], start=True, stop=True)
                last.then_inc(s_mm, 1)

            def max_broadcast(s):
                c = SPANS[s][-1]
                pe.wait_ge(s_mc, c + 1)
                for b in range(QB):
                    last = pe.matmul(PM[:, 0, 0, 128 * b:128 * b + 128],
                                     m_run[c % 2][:, b:b + 1].to_broadcast([128, 128]), ident_r[:, :],
                                     start=True, stop=True)
                last.then_inc(s_bc, 1)

            def score(n):
                c, t = n // TPC, n % TPC
                if t == 0:
                    pe.wait_ge(s_hi, c + 1)
                    pe.wait_ge(s_lo, c + 1)
                    pe.wait_ge(s_row, span_of[c] + 1)
                if n >= 2:
                    pe.wait_ge(s_ex, n - 1)
                keys = slice(TILE * t, TILE * t + TILE)
                S = PS[:, n % 2, :]
                hi, lo, q = ctx_hi[c % RHI], ctx_lo[c % RLO], q_hi[span_of[c] % 2]
                pe.matmul(S, lo[:, keys], q[0:CD, :], start=True, stop=False)
                pe.matmul(S, hi[0:CD, keys], q_lo[:, :], start=False, stop=False)
                pe.matmul(S, hi[:, keys], q[:, :], start=False, stop=True).then_inc(s_sc, 1)

            def sum_values(n):
                c, t = n // TPC, n % TPC
                s = span_of[c]
                first, last = n == tiles_before[s], n == tiles_before[s + 1] - 1
                if t == 0:
                    pe.wait_ge(s_vh, c + 1)
                    pe.wait_ge(s_vl, c + 1)
                if first and s >= 2:
                    pe.wait_ge(s_cb, s - 1)
                pe.wait_ge(s_eh, n + 1)
                O = PO[0:CD + 1, s % 2, :]
                hi, lo = val_hi[c % 2][:, t, :], val_lo[c % 2][:, t, :]
                pe.matmul(O, lo, p_hi[n % 3][:, :], start=first, stop=False)
                pe.matmul(O, hi, p_hi[n % 3][:, :], start=False, stop=False)
                pe.wait_ge(s_pl, n + 1)
                pe.matmul(O, hi, p_lo[n % 3][:, :], start=False, stop=last).then_inc(s_pv, 1)

            pe.wait_ge(s_ones, 6 + RHI + 2)
            pe.wait_ge(s_idr, 1)
            pe.wait_ge(s_qh, 1)
            max_block(0, 0)
            max_block(0, 1)
            pe.wait_ge(s_wv, 32)
            for j in range(2):
                for h in range(4 * j, 4 * j + 4):
                    last = pe.matmul(PS[0:CD, j, DM * (h % 4):DM * (h % 4) + DM], wvT[:, h, :], wo_x[:, h, :],
                                     start=True, stop=True)
                last.then_inc(s_B_ps, 1)
            max_block(0, 2)
            max_block(0, 3)
            max_broadcast(0)
            pe.wait_ge(s_ql, 1)
            pe.wait_ge(s_qh, 2)
            pe.wait_ge(s_B, 2)

            for c in range(NCH):
                for t in range(TPC):
                    n = TPC * c + t
                    score(n)
                    if n >= 2:
                        sum_values(n - 2)
                    for item in max_blocks.get((c, t), []):
                        max_block(*item)
                    if (c, t) in broadcast_after:
                        max_broadcast(broadcast_after[(c, t)])
            for n in range(TPC * NCH - 2, TPC * NCH):
                sum_values(n)

            pe.wait_ge(s_cb, NSP)
            for g in range(XH // 2):
                for a in range(2):
                    h = g + a * XH // 2
                    last = pe.matmul(PM[TOK * a:TOK * a + TOK, g // 2, g % 2, 0:DM + 1],
                                     acc[:, TOK * h:TOK * h + TOK], Bm[:, h, :], start=True, stop=True)
                last.then_inc(s_y, 1)
            pe.wait_ge(s_fold, 1)
            pe.matmul(PS[0:TOK, 1, 0:DM], cst[:, C_FO:C_FO + TOK], xr[XH // 2 - 1][:, :], start=True,
                      stop=True).then_inc(s_x1p, 1)

            def biases(b):
                pe.matmul(PM[:, b // 2, b % 2, :], b1_sb[:, b, :], sel_sb[:, :], start=True, stop=False,
                          skip_group_check=True)

            pe.wait_ge(s_fb, 80)
            biases(0)
            biases(1)
            transpose_normed(2)
            pe.wait_ge(s_xnT, 2)
            pe.wait_ge(s_aw, 48)
            pe.matmul(PO[:, 0, 0:3 * DM], xnT[:, :], wqkv_sb[:, :], start=True, stop=True).then_inc(s_qkv, 1)
            biases(2)
            biases(3)
            pe.wait_ge(s_qkn, 1)
            pe.transpose(PO[:, 1, 64:128], qkn[:, 0:DM], ident[0:TOK, 0:TOK])
            pe.transpose(PO[:, 1, 128:192], qkn[:, DM:2 * DM], ident[0:TOK, 0:TOK]).then_inc(s_qkT, 1)
            pe.wait_ge(s_qm, 1)
            pe.wait_ge(s_km, 2)
            pe.matmul(PS[:, 0, :], qm[:, :, :].rearrange("p a t -> p (a t)"),
                      km[:, :, :].rearrange("p g m -> p (g m)"), start=True, stop=True).then_inc(s_ss, 1)
            pe.wait_ge(s_sp, 1)
            for g in range(4):
                last = pe.transpose(PS[:, 1, 128 * g:128 * g + 128],
                                    pe_[:, 2 * g:2 * g + 2, :].rearrange("p g m -> p (g m)"), ident)
            last.then_inc(s_pt, 1)
            pe.matmul(PS[:, 0, 0:FC * TOK], b1_sb[0:FC, NB, :], sel_sb[0:FC, 0:FC * TOK], start=True, stop=False,
                      skip_group_check=True)
            pe.wait_ge(s_vm, 2)
            pe.wait_ge(s_ptc, 1)
            for g in range(4):
                last = pe.matmul(PO[:, 0, 34 * g:34 * g + 34], pT[:, g, :],
                                 vm[:, 2 * g:2 * g + 2, :].rearrange("p g e -> p (g e)"), start=True, stop=True)
            last.then_inc(s_so, 1)
            pe.wait_ge(s_ao, 2)
            pe.transpose(PO[0:DM // 2, 1, 192:320], ao[:, :, :].rearrange("p g e -> p (g e)"), ident).then_inc(s_aoT, 1)
            pe.wait_ge(s_aoTc, 1)
            for a in range(2):
                last = pe.matmul(PO[0:TOK, 0, 256:384], aoT[:, a, :], woT_sb[:, a, :], start=(a == 0), stop=(a == 1))
            last.then_inc(s_pj, 1)

            transpose_normed(3)
            pe.wait_ge(s_xnT, 3)
            pe.matmul(PO[0:TOK, 0, 384:384 + NE], xnT[:, 0:TOK], wg_sb[:, :], start=True, stop=True).then_inc(s_lg, 1)
            pe.wait_ge(s_fw1, 32)
            for b in [NB] + list(range(NB)):
                blocks = FC if b == NB else 8
                bank = PS[:, 0, :] if b == NB else PM[:, b // 2, b % 2, :]
                for j in range(blocks):
                    e = NE if b == NB else EPB * b + j // FC
                    last = pe.matmul(bank[:, TOK * j:TOK * j + TOK], w1_sb[:, e, 128 * (j % FC):128 * (j % FC) + 128],
                                     xnT[:, 0:TOK], start=False, stop=(j == blocks - 1), skip_group_check=True)
                last.then_inc(s_hid, 1)
            pe.wait_ge(s_cw, 1)
            pe.transpose(PO[0:NE + 1, 0, 0:TOK], cw[:, :], ident[0:TOK, 0:TOK]).then_inc(s_cwT, 1)
            pe.wait_ge(s_cwd, 1)
            pe.matmul(PS[:, 1, :], halves[:, :], cwd[:, :, :].rearrange("p e t -> p (e t)"),
                      start=True, stop=True).then_inc(s_cwb, 1)
            acc_y = PO[0:TOK, 1, 320:320 + DM]
            pe.wait_ge(s_cwTc, 1)
            pe.matmul(acc_y, cwT[:, :], b2_sb[:, :], start=True, stop=False)
            pe.wait_ge(s_fw2, 32)
            pe.wait_ge(s_ws2, 1)
            pe.wait_ge(s_hs, 1)
            for f in range(FC):
                pe.matmul(acc_y, hs[NB][:, TOK * f:TOK * f + TOK], w2_sb[:, NE, f, :], start=False, stop=False)
            for b in range(NB):
                pe.wait_ge(s_hw, b + 1)
                for j in range(8):
                    last = pe.matmul(acc_y, hw[b][:, TOK * j:TOK * j + TOK], w2_sb[:, EPB * b + j // FC, j % FC, :],
                                     start=False, stop=(b == NB - 1 and j == 7))
            last.then_inc(s_yn, 1)


def _constants():
    import numpy as np
    c = np.zeros((128, C_W), np.float32)
    c[:, C_ID:C_ID + 128] = np.eye(128)
    r = np.arange(128)
    h = r // SD
    for g in range(8):
        c[:, C_MR + g] = h % 8 == g
        c[:, C_MV + g] = r // TOK == g % 2
    for a in range(2):
        c[:, C_ML + a] = h // 8 == a
    c[:, C_IO:C_IO + NE] = np.arange(NE)
    c[:, C_FO:C_FO + TOK] = r[:, None] % TOK == np.arange(TOK)
    sel = np.repeat(np.eye(8, dtype=np.float32), TOK, axis=1)
    return c, sel


def kernel(**inputs):
    import numpy as np
    import concourse.bacc as bacc
    from concourse.bass_utils import run_bass_kernel_spmd

    g = {n.removeprefix("L0_"): np.asarray(a) for n, a in inputs.items()}
    ctx = g["ctx_768"][0].reshape(NCH, TILE, TPC, CD)
    v_cols = np.arange(DM).reshape(2, 8, SD).transpose(1, 0, 2).reshape(-1)
    consts, sel = _constants()
    arrays = {
        "x": g["x"][0],
        "ctx_n": ctx,
        "ctx_t": ctx.transpose(3, 0, 2, 1).reshape(CD, NCH, CHUNK),
        "wq_t": g["xattn_Wq"].reshape(DM, XH, XD).transpose(2, 1, 0),
        "wk_t": g["xattn_Wk"].reshape(CD, XH, XD).transpose(2, 1, 0),
        "wv_t": g["xattn_Wv"].reshape(CD, XH, XD).transpose(2, 1, 0),
        "wout": g["xattn_Wout"].reshape(XH, XD, DM).transpose(1, 0, 2),
        "bout": g["xattn_bout"],
        "wqkv": np.concatenate([g["attn_Wq"].T, g["attn_Wk"].T, g["attn_Wv"].T[:, v_cols]], axis=1),
        "wo_t": g["attn_Wo"].T.reshape(2, DM // 2, DM).transpose(1, 0, 2),
        "norm_w": np.stack([np.tile(g["attn_qn_w"], SH), np.tile(g["attn_kn_w"], SH)], axis=1),
        "wg": g["ffn_Wg"],
        "w1": g["ffn_W1"].transpose(1, 0, 2),
        "w2": g["ffn_W2"].reshape(NE, FC, 128, DM).transpose(2, 0, 1, 3),
        "ws1": g["ffn_Ws1"],
        "ws2": g["ffn_Ws2"].reshape(FC, 128, DM).transpose(1, 0, 2),
        "b1_rows": g["ffn_b1"].reshape(NB, 8, 128).transpose(1, 0, 2),
        "bs1_rows": g["ffn_bs1"].reshape(FC, 128),
        "b2_rows": np.concatenate([g["ffn_b2"], g["ffn_bs2"][None]], axis=0),
        "consts": consts,
        "sel8": sel,
    }
    nc = bacc.Bacc("TRN2", target_bir_lowering=False, num_devices=1)
    sent, aps = {}, []
    for name, a in arrays.items():
        a = np.ascontiguousarray(a)
        sent[f"in_{name}"] = a
        aps.append(nc.dram_tensor(f"in_{name}", a.shape, mybir.dt.from_np(a.dtype), kind="ExternalInput").ap())
    out = nc.dram_tensor("out", (TOK, DM), F32, kind="ExternalOutput").ap()
    build(nc, *aps, out)
    result = run_bass_kernel_spmd(nc, [sent], core_ids=[0])
    return result.results[0]["out"].reshape(1, TOK, DM)
```

```python
from contextlib import ExitStack

import concourse.bass as bass
from concourse import mybir

F32 = mybir.dt.float32
F32R = mybir.dt.float32r
BF16 = mybir.dt.bfloat16
U32 = mybir.dt.uint32
ALU = mybir.AluOpType
ACT = mybir.ActivationFunctionType
AX = mybir.AxisListType

TOK, DM = 64, 128
KEYS, CD = 6272, 96
XH, XD = 8, 128
Q = XH * TOK
QB = Q // 128
TILE = 128
TPC = 7
CHUNK = TPC * TILE
NCH = KEYS // CHUNK
R32, RHI, RLO = 3, 4, 3
HALF = CHUNK // 2
XSCALE = 1.5 * XD ** -0.5
SH, SD = 16, 8
NE, FF = 8, 512
FC = FF // 128
EPB = 2
NB = NE // EPB
LN_EPS, RMS_EPS, W_EPS, SHARED = 1e-5, 1.1920928955078125e-07, 1e-9, 0.1
LOWEST = -3.0e38
BROADCAST_AT = TPC - 2
RW1 = 3
SPLIT_SLOTS = [(1, 6)] + [(c, t) for c in range(2, 6) for t in (3, 6)]
MIDDLE_LAG = {3: 3, 6: 2}
WARM = 9

C_ID = 0
C_MR = C_ID + 128
C_ML = C_MR + 8
C_MV = C_ML + 2
C_IO = C_MV + 8
C_FO = C_IO + 8
C_W = C_FO + 128


def build(nc, x, ctx_n, ctx_t, wqk_t, wv_t, wout, bout, wqkv, wo_t, norm_w, wg, w1, w2, ws1, ws2,
          b1_rows, bs1_rows, b2_rows, consts, sel8, out):
    with ExitStack() as ctx:
        def sb(name, shape, dt=F32):
            return ctx.enter_context(nc.sbuf_tensor(name, shape, dt))

        def pb(name, shape, dt=F32):
            return ctx.enter_context(nc.psum_tensor(name, shape, dt))

        def sem(name):
            return ctx.enter_context(nc.semaphore(name))

        x_sb = sb("x_sb", [TOK, DM])
        xb = sb("xb", [TOK, DM])
        warm = sb("warm", [128, 512], BF16)
        bout_b = sb("bout_b", [TOK, DM])
        cst = sb("cst", [128, C_W])
        ident_r = sb("ident_r", [128, 128], F32R)
        expo = sb("expo", [2 * TOK, 1])
        w2_sb = sb("w2_sb", [128, (NE + 1) * FC * DM])

        def early(start, width):
            return w2_sb[:, start:start + XH * width].rearrange("p (h c) -> p h c", h=XH)

        wqk = early(0, DM + CD)
        wvT = early(XH * (DM + CD), CD)
        wo_x = early(XH * (DM + 2 * CD), DM)
        A = early(XH * (2 * DM + 2 * CD), CD)
        Bm = sb("Bm", [CD + 1, XH, DM + 1])
        ctx32 = [sb(f"ctx32_{p}", [CD, CHUNK]) for p in range(R32)]
        ctx_hi = [sb(f"ctx_hi_{p}", [CD + 1, CHUNK], F32R) for p in range(RHI)]
        ctx_lo = [sb(f"ctx_lo_{p}", [CD, CHUNK], F32R) for p in range(RLO)]
        val32 = [sb(f"val32_{p}", [128, TPC, CD + 1]) for p in range(2)]
        val_hi = [sb(f"val_hi_{p}", [128, TPC, CD + 1], F32R) for p in range(2)]
        val_lo = [sb(f"val_lo_{p}", [128, TPC, CD + 1], F32R) for p in range(2)]
        q_hi = [sb(f"q_hi_{p}", [CD + 1, Q], F32R) for p in range(2)]
        q_lo = sb("q_lo", [CD, Q], F32R)
        mx = [sb(f"mx_{p}", [128, QB]) for p in range(2)]
        m_run = [sb(f"m_run_{p}", [128, QB], F32R) for p in range(2)]
        m_row = [sb(f"m_row_{p}", [CD + 1, Q]) for p in range(2)]
        m_diff = sb("m_diff", [CD + 1, Q])
        alpha = sb("alpha", [CD + 1, Q])
        p_hi = [sb(f"p_hi_{i}", [128, Q], F32R) for i in range(3)]
        p_lo = [sb(f"p_lo_{i}", [128, Q], F32R) for i in range(3)]
        p32 = [sb(f"p32_{i}", [128, Q]) for i in range(2)]
        acc = sb("acc", [CD + 1, Q])
        st = sb("st", [2 * TOK, 6])
        mv = sb("mv", [2 * TOK, 2])
        ve = sb("ve", [2 * TOK, 1])
        vee = sb("vee", [TOK, 1])
        rstd = sb("rstd", [2 * TOK, 1])
        xn = sb("xn", [2 * TOK, DM])
        xnT = sb("xnT", [DM, 2 * TOK])
        xr = [sb(f"xr_{i}", [2 * TOK, DM]) for i in range(4)]
        x1 = sb("x1", [TOK, DM])
        rs_x = sb("rs_x", [2 * TOK, XH // 2])
        wqkv_sb = sb("wqkv_sb", [DM, 3 * DM])
        woT_sb = sb("woT_sb", [DM // 2, 2, DM])
        nw = sb("nw", [128, 2])
        wn = sb("wn", [128, 1])
        wmask = sb("wmask", [128, 2])
        sq = sb("sq", [TOK, 2 * DM])
        ms = sb("ms", [TOK, 2 * SH])
        rr = sb("rr", [TOK, 2 * SH])
        qkn = sb("qkn", [TOK, 2 * DM])
        qm = sb("qm", [128, 2, TOK])
        km = sb("km", [128, 8, TOK])
        vm = sb("vm", [128, 8, 17])
        smax = sb("smax", [128, 8])
        rsum = sb("rsum", [128, 8])
        ao = sb("ao", [128, 8, 8])
        aoT = sb("aoT", [DM // 2, 2, TOK])
        x2 = sb("x2", [TOK, DM])
        wg_sb = sb("wg_sb", [DM, NE])
        w1_in = sb("w1_in", [DM, RW1, FF])
        sd = w1_in[:, 0, :].rearrange("p (g m) -> p g m", g=8)
        pe_ = w1_in[:, 1, :].rearrange("p (g m) -> p g m", g=8)
        pT = w1_in[:, 2, :].rearrange("p (g m) -> p g m", g=4)
        w1_rest = [sb(f"w1_rest_{i}", [DM, FF]) for i in range(2)]
        w1_part = [sb(f"w1_part_{i}", [DM, NE + 1, FF], BF16) for i in range(3)]
        x_part = [sb(f"x_part_{i}", [DM, TOK], BF16) for i in range(3)]
        x_rest = sb("x_rest", [DM, TOK])
        w2_hi = sb("w2_hi", [128, NE + 1, FC, DM], F32R)
        w2_lo = sb("w2_lo", [128, NE + 1, FC, DM], F32R)
        b1_sb = sb("b1_sb", [8, NB + 1, 128])
        b2_sb = sb("b2_sb", [NE + 1, DM])
        sel_sb = sb("sel_sb", [8, 8 * TOK])
        nlm = sb("nlm", [TOK, 1])
        le = sb("le", [TOK, NE])
        ls = sb("ls", [TOK, 1])
        lr = sb("lr", [TOK, 1])
        pr = sb("pr", [TOK, NE])
        v8 = sb("v8", [TOK, 8])
        i8 = sb("i8", [TOK, 8], U32)
        if8 = sb("if8", [TOK, 2])
        wsum = sb("wsum", [TOK, 1])
        wr = sb("wr", [TOK, 1])
        w2v = sb("w2v", [TOK, 2])
        c1 = sb("c1", [TOK, NE])
        c2 = sb("c2", [TOK, NE])
        cw = sb("cw", [TOK, NE + 1])
        cwh = sb("cwh", [TOK, NE])
        dummy = sb("table_dummy", [1, 2])
        rroot = sb("rroot", [TOK, 2 * SH])
        cwT = sb("cwT", [NE + 1, TOK])
        th = w1_rest
        hs = p32
        hs_hi = [p_hi[0], p_hi[1], p_hi[2], p_lo[0], p_lo[1]]
        hs_lo = [v[:, :, :].rearrange("p t c -> p (t c)")[:, 0:8 * TOK] for v in val_hi + val_lo] + [p_lo[2]]
        y = [sb(f"y_{i}", [TOK, DM]) for i in range(2)]

        PM = pb("PM", [128, 2, 2, 512])
        PS = pb("PS", [128, 2, 512])
        PO = pb("PO", [128, 2, 512])

        s_x = sem("x_loaded")
        s_cst = sem("consts_loaded")
        s_bout = sem("bout_loaded")
        s_wqk = [sem(f"wqk_{j}_loaded") for j in range(2)]
        s_wv = sem("wv_wout_loaded")
        s_aw = sem("attn_weights_loaded")
        s_w1 = [sem(f"w1_{i}_loaded") for i in range(RW1)]
        s_wh = sem("w1_high_ready")
        s_wm = sem("w1_middle_ready")
        s_wr = [sem("w1_rest_ready"), sem("w1_low_ready")]
        s_xp = sem("x_part_ready")
        s_fw2 = sem("w2_loaded")
        s_fb = sem("ffn_small_loaded")
        s_ct = [sem(f"ctx32_{p}_loaded") for p in range(R32)]
        s_cv = [sem(f"val_{p}_loaded") for p in range(2)]
        s_ones = sem("constants_set")
        s_dz = sem("vector_constants_set")
        s_idr = sem("ident_rounded")
        s_ve = sem("variance_ready")
        s_vee = sem("scaled_epsilon_ready")
        s_pow = sem("inverse_root_ready")
        s_xn = sem("normed_ready")
        s_xnT_ps = sem("normed_transposed")
        s_xnT = sem("normed_T_ready")
        s_A_ps = sem("A_in_psum")
        s_A = sem("A_ready")
        s_B_ps = sem("B_in_psum")
        s_B = sem("B_ready")
        s_q_ps = sem("queries_in_psum")
        s_qh = sem("q_hi_ready")
        s_ql = sem("q_lo_ready")
        s_q32 = sem("queries_copied")
        s_hi = sem("ctx_hi_ready")
        s_lo = sem("ctx_lo_ready")
        s_mm = sem("max_scores_ready")
        s_mr = sem("max_reduced")
        s_bc = sem("max_broadcast_ready")
        s_row = sem("shift_row_ready")
        s_mb = sem("max_row_copied")
        s_mc = sem("chunk_max_ready")
        s_df = sem("max_diff_ready")
        s_al = sem("alpha_ready")
        s_sc = sem("scores_ready")
        s_eh = sem("probs_hi_ready")
        s_ex = sem("probs_ready")
        s_pl = sem("probs_lo_ready")
        s_vh = sem("val_hi_ready")
        s_vl = sem("val_lo_ready")
        s_wz = sem("warm_set")
        s_rs = sem("head_sums_inverted")
        s_fold = [sem("even_heads_scaled"), sem("odd_heads_scaled")]
        s_x1p = sem("x1_in_psum")
        s_rt = sem("roots_ready")
        s_dm = sem("dummy_done")
        s_pv = sem("tile_summed")
        s_am = sem("acc_scaled")
        s_cb = sem("chunk_combined")
        s_y = sem("heads_projected")
        s_x1 = sem("x1_copied")
        s_dve = sem("vector_step")
        s_qk = sem("qk_in_psum")
        s_v = sem("v_in_psum")
        s_sq = sem("squares_ready")
        s_ms = sem("square_sums_ready")
        s_qkn = sem("qk_normed")
        s_qkT = sem("qk_transposed")
        s_qm = sem("q_masked")
        s_km = sem("k_masked")
        s_vm = sem("v_masked")
        s_ss = sem("self_scores_ready")
        s_sd = sem("self_scores_shifted")
        s_sp = sem("self_probs_ready")
        s_pt = sem("self_probs_transposed")
        s_ptc = sem("self_probs_T_ready")
        s_so = sem("self_sums_ready")
        s_ao = sem("self_out_ready")
        s_aoT = sem("self_out_transposed")
        s_aoTc = sem("self_out_T_ready")
        s_pj = sem("self_projected")
        s_x2 = sem("x2_ready")
        s_lg = sem("logits_ready")
        s_nl = sem("logit_max_ready")
        s_le = sem("logit_exp_ready")
        s_cw = sem("gates_ready")
        s_cwT = sem("gates_transposed")
        s_cwTc = sem("gates_T_ready")
        s_cwh = sem("half_gates_ready")
        s_ws2 = sem("ws2_scaled")
        s_hid = sem("hidden_ready")
        s_th = sem("tanh_ready")
        s_hs = sem("silu_ready")
        s_hh = sem("silu_hi_ready")
        s_hl = sem("silu_lo_ready")
        s_w2h = sem("w2_hi_ready")
        s_w2l = sem("w2_lo_ready")
        s_ysh = sem("shared_expert_done")
        s_ye = sem("expert_done")
        s_yt = sem("expert_taken")
        s_fin = sem("result_ready")
        s_out = sem("result_stored")

        ident = cst[:, C_ID:C_ID + 128]
        w2_of = w2_sb[:, :].rearrange("p (e f d) -> p e f d", e=NE + 1, f=FC)
        block = ctx.enter_context(nc.Block())

        Y = [PS[:, 0, 0:DM + 1], PS[:, 1, 0:DM + 1], PO[:, 1, 0:DM + 1], PO[:, 0, 0:DM + 1]]
        x1_ps = PM[:, 1, 1, 0:DM]
        v_ps = PO[:, 1, 192:320]
        self_scores = [PS[:, 0, 0:256], PO[:, 0, 0:256]]
        x2_ps = PO[0:TOK, 0, 256:384]
        y_expert = [PS[0:TOK, 1, 0:DM], PO[0:TOK, 0, 0:DM], PS[0:TOK, 0, 0:DM], PM[0:TOK, 0, 0, 0:DM]]
        y_shared = PO[0:TOK, 1, 320:320 + DM]

        max_blocks = {}
        for c in range(1, NCH):
            for b, slot in enumerate([(c - 2, TPC - 1), (c - 1, 0), (c - 1, 1), (c - 1, 2)]):
                max_blocks[slot] = (c, b)
        split_at, middle_at = {}, {}
        for e, (c, t) in enumerate(SPLIT_SLOTS):
            split_at[c, t] = e
            n = TPC * c + t + MIDDLE_LAG[t]
            middle_at[n // TPC, n % TPC] = e

        @block.sync
        def _(sp):
            sp.dma_start(x_sb[:, :], x).then_inc(s_x, 16)
            sp.dma_start(cst[:, :], consts).then_inc(s_cst, 16)
            sp.dma_start(ctx32[0][:, :], ctx_t[:, 0, :]).then_inc(s_ct[0], 16)
            sp.dma_start(wqk[:, 4:8, :], wqk_t[:, 4:8, :]).then_inc(s_wqk[1], 16)
            sp.dma_start(wvT[:, :, :], wv_t).then_inc(s_wv, 16)
            sp.dma_start(wo_x[:, :, :], wout).then_inc(s_wv, 16)
            sp.dma_start(ctx32[1][:, :], ctx_t[:, 1, :]).then_inc(s_ct[1], 16)
            sp.dma_start(val32[0][:, :, 0:CD], ctx_n[0]).then_inc(s_cv[0], 16)
            sp.dma_start(ctx32[2][:, :], ctx_t[:, 2, :]).then_inc(s_ct[2], 16)
            sp.dma_start(val32[1][:, :, 0:CD], ctx_n[1]).then_inc(s_cv[1], 16)
            sp.dma_start(bout_b[:, :], bout.rearrange("(a n) -> a n", a=1).to_broadcast([TOK, DM])).then_inc(s_bout, 16)
            sp.dma_start(wqkv_sb[:, :], wqkv).then_inc(s_aw, 16)
            sp.dma_start(woT_sb[:, :, :], wo_t).then_inc(s_aw, 16)
            sp.dma_start(nw[:, :], norm_w).then_inc(s_aw, 16)
            sp.dma_start(wg_sb[:, :], wg).then_inc(s_fb, 16)
            sp.dma_start(b1_sb[:, 0:NB, :], b1_rows).then_inc(s_fb, 16)
            sp.dma_start(b1_sb[0:FC, NB, :], bs1_rows).then_inc(s_fb, 16)
            sp.dma_start(b2_sb[:, :], b2_rows).then_inc(s_fb, 16)
            sp.dma_start(sel_sb[:, :], sel8).then_inc(s_fb, 16)

            def load_ctx(c):
                sp.wait_ge(s_hi, c - R32 + 1)
                sp.wait_ge(s_lo, c - R32 + 1)
                sp.dma_start(ctx32[c % R32][:, :], ctx_t[:, c, :]).then_inc(s_ct[c % R32], 16)

            def load_val(c):
                sp.wait_ge(s_vh, c - 1)
                sp.wait_ge(s_vl, c - 1)
                sp.dma_start(val32[c % 2][:, :, 0:CD], ctx_n[c]).then_inc(s_cv[c % 2], 16)

            def load_w1(e):
                if e >= RW1:
                    sp.wait_ge(s_wr[0], e - RW1 + 1)
                sp.dma_start(w1_in[:, e % RW1, :], ws1 if e == NE else w1[:, e, :]).then_inc(s_w1[e % RW1], 16)

            load_ctx(3)
            load_val(2)
            for e in range(RW1):
                load_w1(e)
            sp.wait_ge(s_q_ps, QB)
            sp.wait_ge(s_B_ps, 2)
            sp.dma_start(w2_of[:, 0:NE, :, :], w2).then_inc(s_fw2, 16)
            sp.dma_start(w2_of[:, NE, :, :], ws2).then_inc(s_fw2, 16)
            for c in range(3, NCH):
                if c + 1 < NCH:
                    load_ctx(c + 1)
                load_val(c)
                for e in range(RW1, NE + 1):
                    if SPLIT_SLOTS[e - RW1][0] == c - 3:
                        load_w1(e)
            for e in range(RW1, NE + 1):
                if SPLIT_SLOTS[e - RW1][0] >= NCH - 3:
                    load_w1(e)
            sp.wait_ge(s_fin, 1)
            sp.dma_start(out, y[NE % 2][:, :]).then_inc(s_out, 16)
            sp.wait_ge(s_out, 16)

        @block.gpsimd
        def _(pool):
            fills = [(expo[:, :], -0.5), (Bm[:, :, :], 0.0), (Bm[CD:CD + 1, :, DM:DM + 1], 1.0),
                     (cw[:, NE:NE + 1], SHARED), (vm[:, :, 16:17], 0.0)]
            fills += [(ctx_hi[p][CD:CD + 1, :].bitcast(F32), 1.0) for p in range(RHI)]
            fills += [(val32[p][:, :, CD:CD + 1], 1.0) for p in range(2)]
            def inverse_root(n, rows=TOK):
                pool.wait_ge(s_ve, n)
                pool.tensor_tensor(rstd[0:rows, :], ve[0:rows, :], expo[0:rows, :], ALU.pow).then_inc(s_pow, 1)

            for n, (place, value) in enumerate(fills):
                if n == 2:
                    inverse_root(1)
                pool.memset(place, value).then_inc(s_ones, 1)
                pool.wait_ge(s_ones, n + 1)

            def low_part(c):
                pool.wait_ge(s_hi, c + 1)
                if c >= RLO:
                    pool.wait_ge(s_sc, TPC * (c - RLO + 1))
                pool.tensor_tensor(ctx_lo[c % RLO][:, :], ctx32[c % R32][:, :],
                                   ctx_hi[c % RHI][0:CD, :].bitcast(F32), ALU.subtract).then_inc(s_lo, 1)

            def low_values(c):
                pool.wait_ge(s_vh, c + 1)
                if c >= 2:
                    pool.wait_ge(s_pv, TPC * (c - 1))
                pool.tensor_tensor(val_lo[c % 2][:, :, :], val32[c % 2][:, :, :],
                                   val_hi[c % 2][:, :, :].bitcast(F32), ALU.subtract).then_inc(s_vl, 1)

            def max_change(c):
                pool.wait_ge(s_mb, c + 1)
                if c == 0:
                    pool.wait_ge(s_dz, 3)
                    pool.wait_ge(s_ql, 1)
                if c >= 1:
                    pool.wait_ge(s_al, c)
                pool.tensor_tensor(m_diff[:, :], m_row[1 - c % 2][:, :], m_row[c % 2][:, :],
                                   ALU.subtract).then_inc(s_df, 1)

            low_part(0)
            pool.wait_ge(s_q32, QB)
            pool.wait_ge(s_qh, QB)
            pool.tensor_tensor(q_lo[:, :], m_diff[0:CD, :], q_hi[0][0:CD, :].bitcast(F32),
                               ALU.subtract).then_inc(s_ql, 1)
            low_values(0)
            low_part(1)
            max_change(0)
            low_part(2)

            def rest_of_w1(e):
                pool.wait_ge(s_wh, e + 1)
                if e >= 2:
                    pool.wait_ge(s_wr[1], e - 1)
                pool.tensor_tensor(w1_rest[e % 2][:, :], w1_in[:, e % RW1, :], w1_part[0][:, e, :],
                                   ALU.subtract).then_inc(s_wr[0], 1)

            def low_w1(e):
                pool.wait_ge(s_wm, e + 1)
                pool.tensor_tensor(w1_part[2][:, e, :], w1_rest[e % 2][:, :], w1_part[1][:, e, :],
                                   ALU.subtract).then_inc(s_wr[1], 1)

            for c in range(NCH):
                for t in range(TPC):
                    if (c, t) in middle_at:
                        low_w1(middle_at[c, t])
                    if t == 2 and c + 1 < NCH:
                        low_values(c + 1)
                    if t == 2 and c >= 1 and c + 2 < NCH:
                        low_part(c + 2)
                    if (c, t) in split_at:
                        rest_of_w1(split_at[c, t])
                if c + 1 < NCH:
                    max_change(c + 1)
            def low_w2(e):
                pool.wait_ge(s_w2h, e + 1)
                pool.tensor_tensor(w2_lo[:, e, :, :], w2_of[:, e, :, :], w2_hi[:, e, :, :].bitcast(F32),
                                   ALU.subtract).then_inc(s_w2l, 1)

            for e in range(2):
                low_w2(e)
            inverse_root(2, 2 * TOK)
            for e in range(2, NE + 1):
                low_w2(e)
            inverse_root(3)

        @block.scalar
        def _(act):
            act.dma_start(wqk[:, 0:4, :], wqk_t[:, 0:4, :]).then_inc(s_wqk[0], 16)
            def high_values(c):
                act.wait_ge(s_cv[c % 2], 16 * (c // 2 + 1))
                if c >= 2:
                    act.wait_ge(s_pv, TPC * (c - 1))
                act.activation(val_hi[c % 2][:, :, :], val32[c % 2][:, :, :], ACT.Copy).then_inc(s_vh, 1)

            def finish_A(g):
                act.wait_ge(s_A_ps, g + 1)
                act.activation(A[:, 2 * g:2 * g + 2, :], PS[:, g % 2, 0:2 * CD].rearrange("p (h c) -> p h c", h=2),
                               ACT.Copy, scale=XSCALE).then_inc(s_A, 1)

            def take_queries(g):
                act.wait_ge(s_q_ps, g + 1)
                act.activation(q_hi[0][0:CD, 128 * g:128 * g + 128], PO[0:CD, g % 2, 0:128], ACT.Copy).then_inc(s_qh, 1)
                act.activation(m_diff[0:CD, 128 * g:128 * g + 128], PO[0:CD, g % 2, 0:128], ACT.Copy).then_inc(s_q32, 1)

            finish_A(0)
            finish_A(1)
            take_queries(0)
            take_queries(1)
            finish_A(2)
            finish_A(3)
            take_queries(2)
            take_queries(3)
            act.wait_ge(s_qh, QB)
            act.activation(q_hi[1][0:CD, :], q_hi[0][0:CD, :].bitcast(F32), ACT.Copy).then_inc(s_qh, 1)
            act.wait_ge(s_hi, 1)
            act.wait_ge(s_ct[1], 16)
            act.activation(ctx_hi[1][0:CD, :], ctx32[1][:, :], ACT.Copy).then_inc(s_hi, 1)
            act.wait_ge(s_ones, 5 + RHI + 2)
            high_values(0)

            def take_B(j):
                act.wait_ge(s_B_ps, j + 1)
                act.activation(Bm[0:CD, 4 * j:4 * j + 4, 0:DM], PO[0:CD, j, :].rearrange("p (h c) -> p h c", h=4),
                               ACT.Copy).then_inc(s_B, 1)

            def max_rows(c):
                act.wait_ge(s_bc, c + 1)
                if c >= 2:
                    act.wait_ge(s_sc, TPC * (c - 1))
                    act.wait_ge(s_df, c)
                act.activation(q_hi[c % 2][CD:CD + 1, :], PM[CD:CD + 1, 0, 0, :], ACT.Copy,
                               scale=-1.0).then_inc(s_row, 1)
                act.activation(m_row[c % 2][:, :], PM[0:CD + 1, 0, 0, :], ACT.Copy).then_inc(s_mb, 1)

            def high_w1(e):
                act.wait_ge(s_w1[e % RW1], 16 * (e // RW1 + 1))
                act.activation(w1_part[0][:, e, :], w1_in[:, e % RW1, :], ACT.Copy).then_inc(s_wh, 1)

            def high_w2(e):
                act.activation(w2_hi[:, e, :, :], w2_of[:, e, :, :], ACT.Copy).then_inc(s_w2h, 1)

            take_B(0)
            max_rows(0)
            for c in range(NCH):
                for t in range(TPC):
                    n = TPC * c + t
                    act.wait_ge(s_sc, n + 1)
                    if n >= 3:
                        act.wait_ge(s_pv, n - 2)
                    act.activation(p_hi[n % 3][:, :], PS[:, n % 2, :], ACT.Exp).then_inc(s_eh, 1)
                    if n >= 2:
                        act.wait_ge(s_pl, n - 1)
                    act.activation(p32[n % 2][:, :], PS[:, n % 2, :], ACT.Exp).then_inc(s_ex, 1)
                    if (c, t) == (0, 0):
                        take_B(1)
                    if t == BROADCAST_AT and c + 1 < NCH:
                        max_rows(c + 1)
                    if t == 2 and c + 1 < NCH:
                        high_values(c + 1)
                    if (c, t) in split_at:
                        high_w1(split_at[c, t])
                    if c == NCH - 1 and t in (1, 2):
                        act.wait_ge(s_fw2, 32)
                        high_w2(t - 1)
                    if t == 3:
                        act.wait_ge(s_df, c + 1)
                        if c >= 1:
                            act.wait_ge(s_am, c)
                        act.activation(alpha[:, :], m_diff[:, :], ACT.Exp).then_inc(s_al, 1)
            act.activation(dummy[:, 0:1], cst[0:1, 0:1], ACT.Sqrt).then_inc(s_dm, 1)
            for g in (1, 3):
                act.wait_ge(s_rs, g + 1)
                act.activation(xr[g][:, :], Y[g][:, 0:DM], ACT.Copy, scale=rs_x[:, g:g + 1]).then_inc(s_fold[1], 1)
            for e in range(2, NE - 2):
                high_w2(e)
            act.wait_ge(s_qk, 1)
            act.activation(sq[:, :], PO[0:TOK, 0, 0:2 * DM], ACT.Square).then_inc(s_sq, 1)
            act.wait_ge(s_ms, 1)
            act.wait_ge(s_vee, 1)
            act.activation(rroot[:, :], ms[:, :], ACT.Sqrt, bias=vee[:, 0:1], scale=1.0 / SD).then_inc(s_rt, 1)
            act.activation(dummy[:, 1:2], cst[0:1, 0:1], ACT.Exp).then_inc(s_dm, 1)
            for j in range(2):
                act.wait_ge(s_sd, j + 1)
                act.activation(pe_[:, 4 * j:4 * j + 4, :], sd[:, 4 * j:4 * j + 4, :], ACT.Exp).then_inc(s_sp, 1)
            act.activation(w2_of[:, NE, :, :], w2_of[:, NE, :, :], ACT.Copy, scale=0.5 * SHARED).then_inc(s_ws2, 1)
            high_w2(NE - 2)
            high_w2(NE - 1)
            act.wait_ge(s_ws2, 1)
            high_w2(NE)
            act.wait_ge(s_nl, 1)
            act.activation(le[:, :], PO[0:TOK, 0, 384:384 + NE], ACT.Exp, bias=nlm[:, 0:1],
                           accum_out=ls[:, :]).then_inc(s_le, 1)

            def tanh(n, w, src):
                act.wait_ge(s_hid, n + 1)
                if n >= 2:
                    act.wait_ge(s_hs, n - 1)
                act.activation(th[n % 2][:, 0:w], src, ACT.Tanh, scale=0.5).then_inc(s_th, 1)

            def high_silu(n, w):
                act.wait_ge(s_hs, n + 1)
                act.activation(hs_hi[n][:, 0:w], hs[n % 2][:, 0:w], ACT.Copy).then_inc(s_hh, 1)

            tanh(0, FC * TOK, PS[:, 0, 0:FC * TOK])
            for b in range(NB):
                tanh(b + 1, 8 * TOK, PM[:, b // 2, b % 2, :])
                high_silu(b, FC * TOK if b == 0 else 8 * TOK)
            high_silu(NB, 8 * TOK)

        @block.vector
        def _(dve):
            steps = [0]

            def link(ins):
                steps[0] += 1
                ins.then_inc(s_dve, 1)
                dve.wait_ge(s_dve, steps[0])

            def layer_norm(n, src, copy_to=None):
                link(dve.bn_stats(st[0:TOK, :], src))
                link(dve.bn_aggr(mv[0:TOK, :], st[0:TOK, :]))
                dve.tensor_scalar(ve[0:TOK, :], mv[0:TOK, 1:2], LN_EPS, None, ALU.add).then_inc(s_ve, 1)
                if copy_to is not None:
                    dve.tensor_copy(copy_to, src).then_inc(s_x2, 1)
                dve.wait_ge(s_pow, n)
                dve.tensor_scalar(xn[0:TOK, :], src, mv[0:TOK, 0:1], rstd[0:TOK, 0:1], ALU.subtract,
                                  ALU.mult).then_inc(s_xn, 1)
                dve.wait_ge(s_xnT_ps, n)
                dve.tensor_copy(xnT[:, 0:TOK], PO[:, 1, 0:TOK]).then_inc(s_xnT, 1)
                dve.wait_ge(s_xnT, n)

            dve.memset(warm[:, :], 0.0).then_inc(s_wz, 1)
            dve.memset(m_run[1][:, :].bitcast(F32), LOWEST).then_inc(s_dz, 1)
            dve.memset(m_row[1][:, :], LOWEST).then_inc(s_dz, 1)
            dve.memset(acc[:, :], 0.0).then_inc(s_dz, 1)
            dve.wait_ge(s_x, 16)
            layer_norm(1, x_sb[:, :])

            def high_part(c):
                dve.wait_ge(s_ct[c % R32], 16 * (c // R32 + 1))
                if c >= RHI:
                    dve.wait_ge(s_sc, TPC * (c - RHI + 1))
                dve.tensor_copy(ctx_hi[c % RHI][0:CD, :], ctx32[c % R32][:, :]).then_inc(s_hi, 1)

            def reduce_block(c, b):
                dve.wait_ge(s_mm, QB * c + b + 1)
                if b == 0 and c >= 2:
                    dve.wait_ge(s_mc, c - 1)
                dve.tensor_reduce(mx[c % 2][:, b:b + 1], PM[:, 1 - b % 2, :, 0:HALF], AX.XY, ALU.max).then_inc(s_mr, 1)

            def running_max(c):
                dve.wait_ge(s_mr, QB * (c + 1))
                if c >= 1:
                    dve.wait_ge(s_mc, c)
                if c >= 2:
                    dve.wait_ge(s_bc, c - 1)
                dve.tensor_tensor(m_run[c % 2][:, :], mx[c % 2][:, :], m_run[1 - c % 2][:, :].bitcast(F32),
                                  ALU.max).then_inc(s_mc, 1)

            def low_probs(n):
                dve.wait_ge(s_ex, n + 1)
                if n >= 3:
                    dve.wait_ge(s_pv, n - 2)
                dve.tensor_tensor(p_lo[n % 3][:, :], p32[n % 2][:, :], p_hi[n % 3][:, :].bitcast(F32),
                                  ALU.subtract).then_inc(s_pl, 1)

            def middle_w1(e):
                dve.wait_ge(s_wr[0], e + 1)
                dve.tensor_copy(w1_part[1][:, e, :], w1_rest[e % 2][:, :]).then_inc(s_wm, 1)

            def scale_sums(c):
                dve.wait_ge(s_al, c + 1)
                if c >= 1:
                    dve.wait_ge(s_cb, c)
                dve.tensor_tensor(acc[:, :], acc[:, :], alpha[:, :], ALU.mult).then_inc(s_am, 1)

            def add_sums(c):
                dve.wait_ge(s_am, c + 1)
                dve.wait_ge(s_pv, TPC * (c + 1))
                dve.tensor_tensor(acc[:, :], acc[:, :], PO[0:CD + 1, c % 2, :], ALU.add).then_inc(s_cb, 1)

            dve.wait_ge(s_cst, 16)
            dve.tensor_copy(ident_r[:, :], ident).then_inc(s_idr, 1)
            high_part(0)
            dve.wait_ge(s_dz, 3)
            for b in range(QB):
                reduce_block(0, b)
            running_max(0)
            reduce_block(1, 0)
            for c in range(NCH):
                for t in range(TPC):
                    if (c, t) != (0, 0):
                        low_probs(TPC * c + t)
                    if (c, t) == (0, 4):
                        dve.wait_ge(s_hi, 2)
                        high_part(2)
                    if t == (5 if c == 0 else 4) and c + 3 < NCH:
                        high_part(c + 3)
                    if t == 3 and c >= 1:
                        add_sums(c - 1)
                    if t == 5:
                        scale_sums(c)
                    if (c, t) in max_blocks:
                        of, b = max_blocks[c, t]
                        reduce_block(of, b)
                        if b == QB - 1:
                            running_max(of)
                    if (c, t) == (0, 0):
                        low_probs(0)
                    if (c, t) in middle_at:
                        middle_w1(middle_at[c, t])
                if c == 1:
                    dve.wait_ge(s_bout, 16)
                    dve.tensor_tensor(xb[:, :], x_sb[:, :], bout_b[:, :], ALU.add).then_inc(s_dz, 1)
                    dve.wait_ge(s_aw, 48)
                    link(dve.tensor_tensor(wn[:, :], nw[:, 0:1], nw[:, 1:2], ALU.mult))
                    link(dve.tensor_scalar(wmask[:, :], cst[:, C_ML:C_ML + 2], wn[:, 0:1], SD ** -0.5, ALU.mult,
                                           ALU.mult))
            dve.wait_ge(s_am, NCH)
            dve.wait_ge(s_pv, TPC * NCH)
            for j in range(2):
                half, sums = (v.rearrange("p (a g t) -> p a g t", a=2, g=4)[:, :, 2 * j:2 * j + 2, :]
                              for v in (acc[:, :], PO[0:CD + 1, (NCH - 1) % 2, :]))
                dve.tensor_tensor(half, half, sums, ALU.add).then_inc(s_cb, 1)

            for g in range(XH // 2):
                dve.wait_ge(s_y, g + 1)
                dve.reciprocal(rs_x[:, g:g + 1], Y[g][:, DM:DM + 1]).then_inc(s_rs, 1)
                if g % 2 == 0:
                    dve.wait_ge(s_rs, g + 1)
                    dve.tensor_scalar(xr[g][:, :], Y[g][:, 0:DM], rs_x[:, g:g + 1], None,
                                      ALU.mult).then_inc(s_fold[0], 1)

            dve.wait_ge(s_x1p, 1)
            link(dve.bn_stats(st[:, :], x1_ps))
            link(dve.bn_aggr(mv[:, :], st[:, :]))
            dve.tensor_scalar(xn[:, :], x1_ps, mv[:, 0:1], None, ALU.subtract).then_inc(s_xn, 1)
            dve.tensor_scalar(ve[:, :], mv[:, 1:2], LN_EPS, None, ALU.add).then_inc(s_ve, 1)
            dve.wait_ge(s_ve, 2)
            dve.tensor_scalar(vee[:, :], ve[0:TOK, :], RMS_EPS, None, ALU.mult).then_inc(s_vee, 1)
            dve.tensor_copy(x1[:, :], PM[0:TOK, 1, 1, 0:DM]).then_inc(s_x1, 1)
            dve.wait_ge(s_xnT_ps, 2)
            dve.tensor_copy(xnT[:, :], PO[:, 1, 0:2 * TOK]).then_inc(s_xnT, 1)
            dve.wait_ge(s_sq, 1)
            dve.tensor_reduce(ms[:, :], sq[:, :].rearrange("p (g d) -> p g d", d=SD), AX.X, ALU.add).then_inc(s_ms, 1)
            dve.wait_ge(s_ones, 5 + RHI + 2)
            dve.wait_ge(s_v, 1)
            dve.wait_ge(s_pow, 2)
            dve.scalar_tensor_tensor(out=vm[:, :, 0:16], in0=v_ps.rearrange("p (g e) -> p g e", e=16),
                                     scalar=rstd[:, 0:1], in1=cst[:, C_MV:C_MV + 8, None].to_broadcast([128, 8, 16]),
                                     op0=ALU.mult, op1=ALU.mult).then_inc(s_vm, 1)
            dve.tensor_copy(vm[:, :, 16], cst[:, C_MV:C_MV + 8]).then_inc(s_vm, 1)
            dve.wait_ge(s_rt, 1)
            link(dve.reciprocal(rr[:, :], rroot[:, :]))
            dve.tensor_tensor(qkn[:, :].rearrange("p (g d) -> p g d", d=SD),
                              PO[0:TOK, 0, 0:2 * DM].rearrange("p (g d) -> p g d", d=SD),
                              rr[:, :, None].to_broadcast([TOK, 2 * SH, SD]), ALU.mult).then_inc(s_qkn, 1)
            dve.wait_ge(s_qkT, 1)
            dve.tensor_tensor(qm[:, :, :], PO[:, 1, None, 64:128].to_broadcast([128, 2, TOK]),
                              wmask[:, :, None].to_broadcast([128, 2, TOK]), ALU.mult).then_inc(s_qm, 1)
            for j in range(2):
                dve.tensor_tensor(km[:, 4 * j:4 * j + 4, :], PO[:, 1, None, 128:192].to_broadcast([128, 4, TOK]),
                                  cst[:, C_MR + 4 * j:C_MR + 4 * j + 4, None].to_broadcast([128, 4, TOK]),
                                  ALU.mult).then_inc(s_km, 1)
            for j in range(2):
                g = slice(4 * j, 4 * j + 4)
                S = self_scores[j].rearrange("p (g m) -> p g m", g=4)
                dve.wait_ge(s_ss, j + 1)
                link(dve.tensor_reduce(smax[:, g], S, AX.X, ALU.max))
                dve.tensor_tensor(sd[:, g, :], S, smax[:, g, None].to_broadcast([128, 4, TOK]),
                                  ALU.subtract).then_inc(s_sd, 1)
            for j in range(2):
                dve.wait_ge(s_pt, j + 1)
                src = PS[:, 1, 0:256] if j == 0 else PO[:, 1, 0:256]
                dve.tensor_copy(pT[:, 2 * j:2 * j + 2, :], src.rearrange("p (g m) -> p g m", g=2)).then_inc(s_ptc, 1)
            dve.wait_ge(s_so, 1)
            O = PO[:, 0, 0:8 * 17].rearrange("p (g e) -> p g e", e=17)
            link(dve.reciprocal(rsum[:, :], O[:, :, 16]))
            for a in range(2):
                rows = slice(TOK * a, TOK * a + TOK)
                dve.tensor_tensor(ao[rows, :, :], O[rows, :, SD * a:SD * a + SD],
                                  rsum[rows, :, None].to_broadcast([TOK, 8, SD]), ALU.mult).then_inc(s_ao, 1)
            dve.wait_ge(s_aoT, 1)
            dve.tensor_copy(aoT[:, :, :],
                            PO[0:DM // 2, 1, 192:320].rearrange("p (a t) -> p a t", a=2)).then_inc(s_aoTc, 1)

            dve.wait_ge(s_pj, 1)
            layer_norm(3, x2_ps, copy_to=x2[:, :])
            dve.tensor_copy(x_part[0][:, :], xnT[:, 0:TOK]).then_inc(s_xp, 1)
            dve.wait_ge(s_xp, 1)
            link(dve.tensor_tensor(x_rest[:, :], xnT[:, 0:TOK], x_part[0][:, :], ALU.subtract))
            dve.tensor_copy(x_part[1][:, :], x_rest[:, :]).then_inc(s_xp, 1)
            dve.wait_ge(s_xp, 2)
            dve.tensor_tensor(x_part[2][:, :], x_rest[:, :], x_part[1][:, :], ALU.subtract).then_inc(s_xp, 1)
            dve.wait_ge(s_lg, 1)
            dve.tensor_reduce(nlm[:, :], PO[0:TOK, 0, 384:384 + NE], AX.X, ALU.max, negate=True).then_inc(s_nl, 1)
            dve.wait_ge(s_le, 1)
            link(dve.reciprocal(lr[:, :], ls[:, :]))
            link(dve.tensor_scalar(pr[:, :], le[:, :], lr[:, 0:1], None, ALU.mult))
            link(dve.max(v8[:, :], pr[:, :]))
            dve.max_index(i8[:, :], v8[:, :], pr[:, :]).then_inc(s_dve, 1)
            steps[0] += 1
            link(dve.tensor_scalar(wsum[:, :], v8[:, 0:1], v8[:, 1:2], W_EPS, ALU.add, ALU.add))

            def silu(n, w, src):
                dve.wait_ge(s_th, n + 1)
                if n >= 2:
                    dve.wait_ge(s_hl, n - 1)
                dve.scalar_tensor_tensor(out=hs[n % 2][:, 0:w], in0=th[n % 2][:, 0:w], scalar=1.0, in1=src,
                                         op0=ALU.add, op1=ALU.mult).then_inc(s_hs, 1)

            def low_silu(n, w):
                dve.wait_ge(s_hh, n + 1)
                dve.tensor_tensor(hs_lo[n][:, 0:w], hs[n % 2][:, 0:w], hs_hi[n][:, 0:w].bitcast(F32),
                                  ALU.subtract).then_inc(s_hl, 1)

            def silu_bank(b):
                silu(b + 1, 8 * TOK, PM[:, b // 2, b % 2, :])

            link(dve.reciprocal(wr[:, :], wsum[:, :]))
            dve.tensor_copy(if8[:, :], i8[:, 0:2]).then_inc(s_dve, 1)
            steps[0] += 1
            silu(0, FC * TOK, PS[:, 0, 0:FC * TOK])
            link(dve.tensor_scalar(w2v[:, :], v8[:, 0:2], wr[:, 0:1], None, ALU.mult))
            silu_bank(0)
            dve.tensor_scalar(c1[:, :], cst[0:TOK, C_IO:C_IO + NE], if8[:, 0:1], w2v[:, 0:1], ALU.is_equal,
                              ALU.mult).then_inc(s_dve, 1)
            steps[0] += 1
            link(dve.tensor_scalar(c2[:, :], cst[0:TOK, C_IO:C_IO + NE], if8[:, 1:2], w2v[:, 1:2], ALU.is_equal,
                                   ALU.mult))
            dve.tensor_tensor(cw[:, 0:NE], c1[:, :], c2[:, :], ALU.add).then_inc(s_cw, 1)
            low_silu(0, FC * TOK)
            dve.wait_ge(s_cw, 1)
            dve.tensor_scalar(cwh[:, :], cw[:, 0:NE], 0.5, None, ALU.mult).then_inc(s_cwh, 1)
            silu_bank(1)
            low_silu(1, 8 * TOK)
            dve.wait_ge(s_cwT, 1)
            dve.tensor_copy(cwT[:, :], PO[0:NE + 1, 0, 0:TOK]).then_inc(s_cwTc, 1)
            silu_bank(2)
            low_silu(2, 8 * TOK)
            silu_bank(3)
            low_silu(3, 8 * TOK)

            def take(e):
                dve.wait_ge(s_ye, e + 1)
                dve.wait_ge(s_yt, e + 1)
                ins = dve.scalar_tensor_tensor(out=y[(e + 1) % 2][:, :], in0=y_expert[e % 4], scalar=cwh[:, e:e + 1],
                                               in1=y[e % 2][:, :], op0=ALU.mult, op1=ALU.add)
                ins.then_inc(s_fin if e == NE - 1 else s_yt, 1)

            dve.wait_ge(s_ysh, 1)
            dve.wait_ge(s_x2, 1)
            dve.tensor_tensor(y[0][:, :], x2[:, :], y_shared, ALU.add).then_inc(s_yt, 1)
            dve.wait_ge(s_cwh, 1)
            low_silu(4, 8 * TOK)
            for e in range(NE):
                take(e)

        @block.tensor
        def _(pe):
            def transpose_normed(n, rows=TOK):
                pe.wait_ge(s_xn, n)
                pe.transpose(PO[:, 1, 0:rows], xn[0:rows, :], ident[0:rows, 0:rows]).then_inc(s_xnT_ps, 1)

            pe.wait_ge(s_wz, 1)
            for _ in range(WARM):
                pe.matmul(PM[:, 0, 0, :], warm[:, 0:128], warm[:, :], start=True, stop=True)
            pe.wait_ge(s_cst, 16)
            transpose_normed(1)
            def form_A(g):
                pe.wait_ge(s_wqk[g // 2], 16)
                if g >= 2:
                    pe.wait_ge(s_A, g - 1)
                for h in range(2):
                    last = pe.matmul(PS[:, g % 2, CD * h:CD * h + CD], wqk[:, 2 * g + h, 0:DM],
                                     wqk[:, 2 * g + h, DM:DM + CD], start=True, stop=True)
                last.then_inc(s_A_ps, 1)

            def queries(g):
                if g == 0:
                    pe.wait_ge(s_xnT, 1)
                pe.wait_ge(s_A, g + 1)
                if g >= 2:
                    pe.wait_ge(s_q32, g - 1)
                for h in range(2):
                    last = pe.matmul(PO[0:CD, g % 2, TOK * h:TOK * h + TOK], A[:, 2 * g + h, :], xnT[:, 0:TOK],
                                     start=True, stop=True)
                last.then_inc(s_q_ps, 1)

            form_A(0)
            form_A(1)
            queries(0)
            queries(1)

            def max_block(c, b):
                if b == 0:
                    pe.wait_ge(s_hi, c + 1)
                if c == 0:
                    pe.wait_ge(s_qh, b + 1)
                if b == 1 and c >= 1:
                    pe.wait_ge(s_row, c)
                    pe.wait_ge(s_mb, c)
                if QB * c + b >= 2:
                    pe.wait_ge(s_mr, QB * c + b - 1)
                for j in range(2):
                    last = pe.matmul(PM[:, 1 - b % 2, j, 0:HALF], q_hi[0][0:CD, 128 * b:128 * b + 128],
                                     ctx_hi[c % RHI][0:CD, HALF * j:HALF * j + HALF], start=True, stop=True)
                last.then_inc(s_mm, 1)

            def max_broadcast(c):
                pe.wait_ge(s_mc, c + 1)
                for b in range(QB):
                    last = pe.matmul(PM[0:CD + 1, 0, 0, 128 * b:128 * b + 128],
                                     m_run[c % 2][:, b:b + 1].to_broadcast([128, CD + 1]), ident_r[:, :],
                                     start=True, stop=True)
                last.then_inc(s_bc, 1)

            def score(n):
                c, t = n // TPC, n % TPC
                if t == 0:
                    pe.wait_ge(s_hi, c + 1)
                    pe.wait_ge(s_lo, c + 1)
                if n >= 2:
                    pe.wait_ge(s_ex, n - 1)
                keys = slice(TILE * t, TILE * t + TILE)
                S = PS[:, n % 2, :]
                hi, lo, q = ctx_hi[c % RHI], ctx_lo[c % RLO], q_hi[c % 2]
                pe.matmul(S, lo[:, keys], q[0:CD, :], start=True, stop=False)
                pe.matmul(S, hi[0:CD, keys], q_lo[:, :], start=False, stop=False)
                if t == 0:
                    pe.wait_ge(s_row, c + 1)
                pe.matmul(S, hi[:, keys], q[:, :], start=False, stop=True).then_inc(s_sc, 1)

            def sum_values(n):
                c, t = n // TPC, n % TPC
                if t == 0:
                    pe.wait_ge(s_vh, c + 1)
                    pe.wait_ge(s_vl, c + 1)
                    if c < 2:
                        pe.wait_ge(s_B, c + 1)
                    if c >= 2:
                        pe.wait_ge(s_cb, c - 1)
                pe.wait_ge(s_eh, n + 1)
                O = PO[0:CD + 1, c % 2, :]
                hi, lo = val_hi[c % 2][:, t, :], val_lo[c % 2][:, t, :]
                pe.matmul(O, lo, p_hi[n % 3][:, :], start=(t == 0), stop=False)
                pe.matmul(O, hi, p_hi[n % 3][:, :], start=False, stop=False)
                pe.wait_ge(s_pl, n + 1)
                pe.matmul(O, hi, p_lo[n % 3][:, :], start=False, stop=(t == TPC - 1)).then_inc(s_pv, 1)

            def form_B():
                for h in range(XH):
                    last = pe.matmul(PO[0:CD, h // 4, DM * (h % 4):DM * (h % 4) + DM], wvT[:, h, :], wo_x[:, h, :],
                                     start=True, stop=True)
                    if h % 4 == 3:
                        last.then_inc(s_B_ps, 1)

            max_block(0, 0)
            form_A(2)
            form_A(3)
            max_block(0, 1)
            queries(2)
            queries(3)
            max_block(0, 2)
            max_block(0, 3)
            pe.wait_ge(s_wv, 32)
            pe.wait_ge(s_q32, QB)
            form_B()
            max_block(1, 0)
            pe.wait_ge(s_ones, 5 + RHI + 2)
            pe.wait_ge(s_idr, 1)
            max_broadcast(0)
            pe.wait_ge(s_ql, 1)
            pe.wait_ge(s_qh, QB + 1)
            pe.wait_ge(s_A, QB)

            for c in range(NCH):
                for t in range(TPC):
                    n = TPC * c + t
                    score(n)
                    if n >= 2:
                        sum_values(n - 2)
                    if (c, t) in max_blocks:
                        max_block(*max_blocks[c, t])
                    if t == BROADCAST_AT and c + 1 < NCH:
                        max_broadcast(c + 1)
            for n in range(TPC * NCH - 2, TPC * NCH):
                sum_values(n)

            def biases(b):
                pe.matmul(PM[:, b // 2, b % 2, :], b1_sb[:, b, :], sel_sb[:, :], start=True, stop=False,
                          skip_group_check=True)

            def fill_pause(n, fresh=False):
                for _ in range(n):
                    pe.matmul(PM[:, 0, 1, :], warm[:, 0:128], warm[:, :], start=fresh, stop=fresh,
                              skip_group_check=not fresh)

            fold = cst[:, C_FO:C_FO + 128]
            pe.wait_ge(s_mb, NCH)
            pe.wait_ge(s_mr, QB * NCH)
            pe.wait_ge(s_dz, 4)
            pe.matmul(x1_ps, fold[0:TOK, :], xb[:, :], start=True, stop=False)
            fill_pause(4, fresh=True)
            pe.wait_ge(s_ex, TPC * NCH)
            for g in range(XH // 2):
                if g % 2 == 0:
                    pe.wait_ge(s_cb, NCH + g // 2)
                for a in range(2):
                    h = g + a * XH // 2
                    last = pe.matmul(Y[g][TOK * a:TOK * a + TOK, :], acc[:, TOK * h:TOK * h + TOK], Bm[:, h, :],
                                     start=True, stop=True)
                last.then_inc(s_y, 1)
            for g in range(XH // 2):
                pe.wait_ge(s_fold[g % 2], g // 2 + 1)
                last = pe.matmul(x1_ps, fold, xr[g][:, :], start=False, stop=(g == XH // 2 - 1))
            last.then_inc(s_x1p, 1)
            pe.wait_ge(s_fb, 80)
            biases(1)

            transpose_normed(2, 2 * TOK)
            pe.wait_ge(s_xnT, 2)
            pe.wait_ge(s_aw, 48)
            pe.matmul(PO[:, 0, 0:2 * DM], xnT[:, :], wqkv_sb[:, 0:2 * DM], start=True, stop=True).then_inc(s_qk, 1)
            pe.matmul(v_ps, xnT[:, :], wqkv_sb[:, 2 * DM:3 * DM], start=True, stop=True).then_inc(s_v, 1)
            biases(2)
            fill_pause(3)
            pe.wait_ge(s_qkn, 1)
            pe.transpose(PO[:, 1, 64:128], qkn[:, 0:DM], ident[0:TOK, 0:TOK])
            pe.transpose(PO[:, 1, 128:192], qkn[:, DM:2 * DM], ident[0:TOK, 0:TOK]).then_inc(s_qkT, 1)
            fill_pause(2)
            pe.wait_ge(s_qm, 1)
            for j in range(2):
                pe.wait_ge(s_km, j + 1)
                pe.matmul(self_scores[j], qm[:, :, :].rearrange("p a t -> p (a t)"),
                          km[:, 4 * j:4 * j + 4, :].rearrange("p g m -> p (g m)"), start=True,
                          stop=True).then_inc(s_ss, 1)
            pe.wait_ge(s_x1, 1)
            biases(3)
            fill_pause(4)
            for j in range(2):
                pe.wait_ge(s_sp, j + 1)
                for g in range(2 * j, 2 * j + 2):
                    bank = PS[:, 1, :] if j == 0 else PO[:, 1, :]
                    last = pe.transpose(bank[:, 128 * (g % 2):128 * (g % 2) + 128],
                                        pe_[:, 2 * g:2 * g + 2, :].rearrange("p g m -> p (g m)"), ident)
                last.then_inc(s_pt, 1)
            pe.matmul(PS[:, 0, 0:FC * TOK], b1_sb[0:FC, NB, :], sel_sb[0:FC, 0:FC * TOK], start=True, stop=False,
                      skip_group_check=True)
            pe.wait_ge(s_vm, 2)
            for g in range(4):
                if g % 2 == 0:
                    pe.wait_ge(s_ptc, g // 2 + 1)
                last = pe.matmul(PO[:, 0, 34 * g:34 * g + 34], pT[:, g, :],
                                 vm[:, 2 * g:2 * g + 2, :].rearrange("p g e -> p (g e)"), start=True, stop=True)
            last.then_inc(s_so, 1)
            fill_pause(3)
            pe.wait_ge(s_ao, 2)
            pe.transpose(PO[0:DM // 2, 1, 192:320], ao[:, :, :].rearrange("p g e -> p (g e)"), ident).then_inc(s_aoT, 1)
            pe.matmul(x2_ps, ident[0:TOK, 0:TOK], x1[:, :], start=True, stop=False)
            pe.wait_ge(s_aoTc, 1)
            for a in range(2):
                last = pe.matmul(x2_ps, aoT[:, a, :], woT_sb[:, a, :], start=False, stop=(a == 1))
            last.then_inc(s_pj, 1)

            biases(0)
            fill_pause(6)
            transpose_normed(3)
            pe.wait_ge(s_xnT, 3)
            pe.matmul(PO[0:TOK, 0, 384:384 + NE], xnT[:, 0:TOK], wg_sb[:, :], start=True, stop=True).then_inc(s_lg, 1)
            pe.wait_ge(s_wh, NE + 1)
            pe.wait_ge(s_wr[1], NE + 1)
            for b in [NB] + list(range(NB)):
                count = FC if b == NB else 8
                bank = PS[:, 0, :] if b == NB else PM[:, b // 2, b % 2, :]
                for xp in range(3):
                    pe.wait_ge(s_xp, xp + 1)
                    for j in range(count):
                        e = NE if b == NB else EPB * b + j // FC
                        for wp in range(3 - xp):
                            last = pe.matmul(bank[:, TOK * j:TOK * j + TOK],
                                             w1_part[wp][:, e, 128 * (j % FC):128 * (j % FC) + 128],
                                             x_part[xp][:, :], start=False, stop=(j == count - 1 and xp == 2),
                                             skip_group_check=True)
                last.then_inc(s_hid, 1)
                if b == NB - 2:
                    pe.wait_ge(s_cw, 1)
                    pe.transpose(PO[0:NE + 1, 0, 0:TOK], cw[:, :], ident[0:TOK, 0:TOK]).then_inc(s_cwT, 1)

            def second_layer(place, n, j, e, f, first, last):
                hi, lo = hs_hi[n][:, TOK * j:TOK * j + TOK], hs_lo[n][:, TOK * j:TOK * j + TOK]
                pe.matmul(place, hi, w2_hi[:, e, f, :], start=first, stop=False)
                pe.matmul(place, hi, w2_lo[:, e, f, :], start=False, stop=False)
                return pe.matmul(place, lo, w2_hi[:, e, f, :], start=False, stop=last)

            pe.wait_ge(s_w2h, NE + 1)
            pe.wait_ge(s_w2l, NE + 1)
            pe.wait_ge(s_hl, 1)
            for f in range(FC):
                second_layer(y_shared, 0, f, NE, f, f == 0, False)
            pe.wait_ge(s_cwTc, 1)
            pe.matmul(y_shared, cwT[:, :], b2_sb[:, :], start=False, stop=True).then_inc(s_ysh, 1)
            for e in range(NE):
                b = e // EPB
                pe.wait_ge(s_hl, b + 2)
                if e >= 4:
                    pe.wait_ge(s_yt, e - 2)
                for f in range(FC):
                    last = second_layer(y_expert[e % 4], b + 1, FC * (e % EPB) + f, e, f, f == 0, f == FC - 1)
                last.then_inc(s_ye, 1)


def _constants():
    import numpy as np
    c = np.zeros((128, C_W), np.float32)
    c[:, C_ID:C_ID + 128] = np.eye(128)
    r = np.arange(128)
    h = r // SD
    for g in range(8):
        c[:, C_MR + g] = h % 8 == g
        c[:, C_MV + g] = r // TOK == g % 2
    for a in range(2):
        c[:, C_ML + a] = h // 8 == a
    c[:, C_IO:C_IO + NE] = np.arange(NE)
    c[:, C_FO:C_FO + 128] = r[:, None] % TOK == r % TOK
    sel = np.repeat(np.eye(8, dtype=np.float32), TOK, axis=1)
    return c, sel


def kernel(**inputs):
    import numpy as np
    import concourse.bacc as bacc
    from concourse.bass_utils import run_bass_kernel_spmd

    g = {n.removeprefix("L0_"): np.asarray(a) for n, a in inputs.items()}
    ctx = g["ctx_768"][0].reshape(NCH, TILE, TPC, CD)
    v_cols = np.arange(DM).reshape(2, 8, SD).transpose(1, 0, 2).reshape(-1)
    consts, sel = _constants()
    arrays = {
        "x": g["x"][0],
        "ctx_n": ctx,
        "ctx_t": ctx.transpose(3, 0, 2, 1).reshape(CD, NCH, CHUNK),
        "wqk_t": np.concatenate([g["xattn_Wq"].reshape(DM, XH, XD), g["xattn_Wk"].reshape(CD, XH, XD)],
                                axis=0).transpose(2, 1, 0),
        "wv_t": g["xattn_Wv"].reshape(CD, XH, XD).transpose(2, 1, 0),
        "wout": g["xattn_Wout"].reshape(XH, XD, DM).transpose(1, 0, 2),
        "bout": g["xattn_bout"],
        "wqkv": np.concatenate([g["attn_Wq"].T, g["attn_Wk"].T, g["attn_Wv"].T[:, v_cols]], axis=1),
        "wo_t": g["attn_Wo"].T.reshape(2, DM // 2, DM).transpose(1, 0, 2),
        "norm_w": np.stack([np.tile(g["attn_qn_w"], SH), np.tile(g["attn_kn_w"], SH)], axis=1),
        "wg": g["ffn_Wg"],
        "w1": g["ffn_W1"].transpose(1, 0, 2),
        "w2": g["ffn_W2"].reshape(NE, FC, 128, DM).transpose(2, 0, 1, 3),
        "ws1": g["ffn_Ws1"],
        "ws2": g["ffn_Ws2"].reshape(FC, 128, DM).transpose(1, 0, 2),
        "b1_rows": g["ffn_b1"].reshape(NB, 8, 128).transpose(1, 0, 2),
        "bs1_rows": g["ffn_bs1"].reshape(FC, 128),
        "b2_rows": np.concatenate([g["ffn_b2"], g["ffn_bs2"][None]], axis=0),
        "consts": consts,
        "sel8": sel,
    }
    nc = bacc.Bacc("TRN2", target_bir_lowering=False, num_devices=1)
    sent, aps = {}, []
    for name, a in arrays.items():
        a = np.ascontiguousarray(a)
        sent[f"in_{name}"] = a
        aps.append(nc.dram_tensor(f"in_{name}", a.shape, mybir.dt.from_np(a.dtype), kind="ExternalInput").ap())
    out = nc.dram_tensor("out", (TOK, DM), F32, kind="ExternalOutput").ap()
    build(nc, *aps, out)
    result = run_bass_kernel_spmd(nc, [sent], core_ids=[0])
    return result.results[0]["out"].reshape(1, TOK, DM)
```
